# Optimizing a Trainium2 kernel written in Bass

```python
import numpy as np
import jax
import jax.numpy as jnp

def _softmax(x, axis=-1):
    return jax.nn.softmax(x, axis=axis)

def _gelu(x):
    return jax.nn.gelu(x, approximate=True)

def _silu(x):
    return jax.nn.silu(x)

def _sigmoid(x):
    return jax.nn.sigmoid(x)

def _layernorm(x, axis=-1, eps=1e-05):
    m = jnp.mean(x, axis=axis, keepdims=True)
    v = jnp.var(x, axis=axis, keepdims=True)
    return (x - m) / jnp.sqrt(v + eps)

def _scatter_add(tgt, idx, src, axis=0):
    return tgt.at[idx].add(src)

def _segment_sum(src, seg, n):
    return jax.ops.segment_sum(src, seg, n)
kernel_name = 'mk_gnn_resnorm_d2_gnn_r8_65d094'

def setup_inputs(seed: int=0):
    np.random.seed(seed)
    _w = jnp.asarray

    def _rec_inputs():
        import jax
        import jax.numpy as jnp
        _gk = jax.random.key(seed)
        x = -0.0005121 + 1.001 * jax.random.normal(jax.random.fold_in(_gk, 1), (12500, 32), jnp.float32)
        src = jax.random.randint(jax.random.fold_in(_gk, 2), (400000,), 0, 12500, jnp.int32)
        dst = jnp.minimum((12500 * jax.random.uniform(jax.random.fold_in(_gk, 3), (400000,)) ** 2.0).astype(jnp.int32), 99999)
        _o = jnp.argsort(dst, stable=True)
        src = src[_o]
        dst = dst[_o]
        edge_attr_3 = 0.000844983 + 0.999762 * jax.random.normal(jax.random.fold_in(_gk, 11), (400000, 3), jnp.float32)
        edge_attr_4 = 0.000398945 + 1.00003 * jax.random.normal(jax.random.fold_in(_gk, 12), (400000, 4), jnp.float32)
        edge_weight = jax.random.uniform(jax.random.fold_in(_gk, 14), (400000,), jnp.float32, 0.0, 1)
        return (x, src, dst, edge_attr_3, edge_attr_4, edge_weight)
    x, src, dst, edge_attr_3, edge_attr_4, edge_weight = _rec_inputs()

    def _L0_gnn_setup():
        import jax, jax.numpy as jnp
        import numpy as np
        N_NODES = 12500
        N_EDGES = 200000
        IN_DIM = 32
        HID = 64
        OUT_DIM = 32
        EDGE_DIM = 4
        key = jax.random.key(seed)
        ks = jax.random.split(key, 12)
        x = jax.random.normal(ks[0], (N_NODES, IN_DIM), dtype=jnp.float32)
        edge_index = jax.random.randint(ks[1], (2, N_EDGES), 0, N_NODES, dtype=jnp.int32)
        edge_attr = jax.random.normal(ks[2], (N_EDGES, EDGE_DIM), dtype=jnp.float32)

        def lin(k, fan_in, fan_out):
            kw, kb = jax.random.split(k)
            bound = 1.0 / np.sqrt(fan_in)
            W = jax.random.uniform(kw, (fan_in, fan_out), minval=-bound, maxval=bound, dtype=jnp.float32)
            b = jax.random.uniform(kb, (fan_out,), minval=-bound, maxval=bound, dtype=jnp.float32)
            return (W, b)
        W1, b1 = lin(ks[3], 2 * IN_DIM, HID)
        W2, b2 = lin(ks[4], HID, 2 * HID)
        W3, b3 = lin(ks[5], 2 * HID, HID)
        W4, b4 = lin(ks[6], HID, OUT_DIM)
        return {'x': x, 'edge_index': edge_index, 'edge_attr': edge_attr, 'W1': W1, 'b1': b1, 'W2': W2, 'b2': b2, 'W3': W3, 'b3': b3, 'W4': W4, 'b4': b4}
    _L0_gnn_all = _L0_gnn_setup()
    _L0_gnn_in = {k: v for k, v in _L0_gnn_all.items() if k in ('W1', 'b1', 'W2', 'b2', 'W3', 'b3', 'W4', 'b4')}
    del _L0_gnn_all

    def _L1_gnn_setup():
        import jax, jax.numpy as jnp
        import numpy as np
        from math import factorial, pi, sqrt
        MUL = 8
        RS = [(MUL, 0), (MUL, 1)]
        N_NODES = 2500
        N_EDGES = 80000
        FEAT_DIM = sum((m * (2 * l + 1) for m, l in RS))
        R_DIM = sum((mo * mi * (2 * min(lo, li) + 1) for mo, lo in RS for mi, li in RS))
        HIDDEN = 64

        def _cg(j1, j2, j3, m1, m2, m3):
            if m1 + m2 != m3:
                return 0.0
            f = factorial
            pre = sqrt((2 * j3 + 1) * f(j3 + j1 - j2) * f(j3 - j1 + j2) * f(j1 + j2 - j3) / f(j1 + j2 + j3 + 1))
            pre *= sqrt(f(j3 + m3) * f(j3 - m3) * f(j1 - m1) * f(j1 + m1) * f(j2 - m2) * f(j2 + m2))
            kmin = max(0, j2 - j3 - m1, j1 - j3 + m2)
            kmax = min(j1 + j2 - j3, j1 - m1, j2 + m2)
            s = 0.0
            for k in range(kmin, kmax + 1):
                s += (-1) ** k / (f(k) * f(j1 + j2 - j3 - k) * f(j1 - m1 - k) * f(j2 + m2 - k) * f(j3 - j2 + m1 + k) * f(j3 - j1 - m2 + k))
            return pre * s

        def _w3j_complex(l1, l2, l3):
            w = np.zeros((2 * l1 + 1, 2 * l2 + 1, 2 * l3 + 1))
            for m1 in range(-l1, l1 + 1):
                for m2 in range(-l2, l2 + 1):
                    m3 = -(m1 + m2)
                    if abs(m3) <= l3:
                        w[m1 + l1, m2 + l2, m3 + l3] = (-1) ** (l1 - l2 - m3) / sqrt(2 * l3 + 1) * _cg(l1, l2, l3, m1, m2, -m3)
            return w

        def _A(l):
            A = np.zeros((2 * l + 1, 2 * l + 1), dtype=complex)
            A[l, l] = 1.0
            for m in range(1, l + 1):
                A[l + m, l + m] = (-1) ** m / sqrt(2)
                A[l + m, l - m] = 1.0 / sqrt(2)
                A[l - m, l - m] = 1j / sqrt(2)
                A[l - m, l + m] = -1j * (-1) ** m / sqrt(2)
            return A

        def real_w3j(l1, l2, l3):
            wc = _w3j_complex(l1, l2, l3).astype(complex)
            wr = np.einsum('abc,ma,nb,oc->mno', wc, _A(l1).conj(), _A(l2).conj(), _A(l3).conj())
            i = int(np.argmax(np.abs(wr)))
            ph = wr.flat[i] / abs(wr.flat[i])
            wr = wr / ph
            assert np.abs(wr.imag).max() < 1e-10
            return np.real(wr).astype(np.float32)
        _W3J = {}
        for _mo, _lo in RS:
            for _mi, _li in RS:
                for _lf in range(abs(_lo - _li), _lo + _li + 1):
                    if (_lo, _lf, _li) not in _W3J:
                        _W3J[_lo, _lf, _li] = jnp.asarray(real_w3j(_lo, _lf, _li))
        _NORM = []
        for _mo, _lo in RS:
            _num = sum((mi * (2 * min(_lo, li) + 1) for mi, li in RS))
            _NORM.append(sqrt(4.0 * pi) * sqrt(2.0 * _lo + 1.0) / sqrt(_num))
        _F_OFFS = [0] + list(np.cumsum([mi * (2 * li + 1) for mi, li in RS]))

        def spherical_harmonics(rel_vec):
            r = rel_vec / jnp.linalg.norm(rel_vec, axis=-1, keepdims=True)
            x, y, z = (r[:, 0], r[:, 1], r[:, 2])
            y0 = jnp.full_like(x, 0.5 / sqrt(pi))[:, None]
            c1 = sqrt(3.0 / (4.0 * pi))
            y1 = c1 * jnp.stack([y, z, x], axis=-1)
            c2a = 0.5 * sqrt(15.0 / pi)
            c2b = 0.25 * sqrt(5.0 / pi)
            c2c = 0.25 * sqrt(15.0 / pi)
            y2 = jnp.stack([c2a * x * y, c2a * y * z, c2b * (3.0 * z * z - 1.0), c2a * x * z, c2c * (x * x - y * y)], axis=-1)
            return jnp.concatenate([y0, y1, y2], axis=-1)
        key = jax.random.key(seed)
        ks = jax.random.split(key, 6)
        features = jax.random.normal(ks[0], (N_NODES, FEAT_DIM), dtype=jnp.float32)
        abs_distances = jax.random.uniform(ks[1], (N_EDGES,), dtype=jnp.float32, minval=0.1, maxval=1.0)
        rel_vec = jax.random.normal(ks[2], (N_EDGES, 3), dtype=jnp.float32)
        edge_index = jax.random.randint(ks[3], (2, N_EDGES), 0, N_NODES, dtype=jnp.int32)
        w1 = jax.random.normal(ks[4], (1, HIDDEN), dtype=jnp.float32)
        b1 = jnp.zeros((HIDDEN,), jnp.float32)
        w2 = jax.random.normal(ks[5], (HIDDEN, R_DIM), dtype=jnp.float32) / sqrt(HIDDEN)
        b2 = jnp.zeros((R_DIM,), jnp.float32)
        return {'features': features, 'abs_distances': abs_distances, 'rel_vec': rel_vec, 'edge_index': edge_index, 'w1': w1, 'b1': b1, 'w2': w2, 'b2': b2}
    _L1_gnn_all = _L1_gnn_setup()
    _L1_gnn_in = {k: v for k, v in _L1_gnn_all.items() if k in ('w1', 'b1', 'w2', 'b2')}
    del _L1_gnn_all
    return {'x': x, 'src': src, 'dst': dst, 'edge_attr_3': edge_attr_3, 'edge_attr_4': edge_attr_4, 'edge_weight': edge_weight, 'L0_gnn_W1': _L0_gnn_in['W1'], 'L0_gnn_b1': _L0_gnn_in['b1'], 'L0_gnn_W2': _L0_gnn_in['W2'], 'L0_gnn_b2': _L0_gnn_in['b2'], 'L0_gnn_W3': _L0_gnn_in['W3'], 'L0_gnn_b3': _L0_gnn_in['b3'], 'L0_gnn_W4': _L0_gnn_in['W4'], 'L0_gnn_b4': _L0_gnn_in['b4'], 'L1_gnn_w1': _L1_gnn_in['w1'], 'L1_gnn_b1': _L1_gnn_in['b1'], 'L1_gnn_w2': _L1_gnn_in['w2'], 'L1_gnn_b2': _L1_gnn_in['b2']}

def reference(x, src, dst, edge_attr_3, edge_attr_4, edge_weight, L0_gnn_W1, L0_gnn_b1, L0_gnn_W2, L0_gnn_b2, L0_gnn_W3, L0_gnn_b3, L0_gnn_W4, L0_gnn_b4, L1_gnn_w1, L1_gnn_b1, L1_gnn_w2, L1_gnn_b2):
    import jax
    import jax.numpy as jnp

    def _L0_gnn_ref(x, edge_index, edge_attr, W1, b1, W2, b2, W3, b3, W4, b4):
        import jax, jax.numpy as jnp
        import numpy as np
        N_NODES = 12500
        N_EDGES = 200000
        IN_DIM = 32
        HID = 64
        OUT_DIM = 32
        EDGE_DIM = 4
        j_idx = edge_index[0]
        i_idx = edge_index[1]
        x_j = x[j_idx]
        x_i = x[i_idx]
        msg = jnp.concatenate([x_i, x_j - x_i], axis=-1)
        h = jax.nn.relu(msg @ W1 + b1)
        h = jax.nn.relu(h @ W2 + b2)
        h = jax.nn.relu(h @ W3 + b3)
        m = h @ W4 + b4
        s = jax.ops.segment_sum(m, i_idx, num_segments=N_NODES)
        cnt = jax.ops.segment_sum(jnp.ones((m.shape[0],), m.dtype), i_idx, num_segments=N_NODES)
        return s / jnp.maximum(cnt, 1.0)[:, None]

    def _L1_gnn_ref(features, abs_distances, rel_vec, edge_index, w1, b1, w2, b2):
        import jax, jax.numpy as jnp
        import numpy as np
        from math import factorial, pi, sqrt
        MUL = 8
        RS = [(MUL, 0), (MUL, 1)]
        N_NODES = 2500
        N_EDGES = 80000
        FEAT_DIM = sum((m * (2 * l + 1) for m, l in RS))
        R_DIM = sum((mo * mi * (2 * min(lo, li) + 1) for mo, lo in RS for mi, li in RS))
        HIDDEN = 64

        def _cg(j1, j2, j3, m1, m2, m3):
            if m1 + m2 != m3:
                return 0.0
            f = factorial
            pre = sqrt((2 * j3 + 1) * f(j3 + j1 - j2) * f(j3 - j1 + j2) * f(j1 + j2 - j3) / f(j1 + j2 + j3 + 1))
            pre *= sqrt(f(j3 + m3) * f(j3 - m3) * f(j1 - m1) * f(j1 + m1) * f(j2 - m2) * f(j2 + m2))
            kmin = max(0, j2 - j3 - m1, j1 - j3 + m2)
            kmax = min(j1 + j2 - j3, j1 - m1, j2 + m2)
            s = 0.0
            for k in range(kmin, kmax + 1):
                s += (-1) ** k / (f(k) * f(j1 + j2 - j3 - k) * f(j1 - m1 - k) * f(j2 + m2 - k) * f(j3 - j2 + m1 + k) * f(j3 - j1 - m2 + k))
            return pre * s

        def _w3j_complex(l1, l2, l3):
            w = np.zeros((2 * l1 + 1, 2 * l2 + 1, 2 * l3 + 1))
            for m1 in range(-l1, l1 + 1):
                for m2 in range(-l2, l2 + 1):
                    m3 = -(m1 + m2)
                    if abs(m3) <= l3:
                        w[m1 + l1, m2 + l2, m3 + l3] = (-1) ** (l1 - l2 - m3) / sqrt(2 * l3 + 1) * _cg(l1, l2, l3, m1, m2, -m3)
            return w

        def _A(l):
            A = np.zeros((2 * l + 1, 2 * l + 1), dtype=complex)
            A[l, l] = 1.0
            for m in range(1, l + 1):
                A[l + m, l + m] = (-1) ** m / sqrt(2)
                A[l + m, l - m] = 1.0 / sqrt(2)
                A[l - m, l - m] = 1j / sqrt(2)
                A[l - m, l + m] = -1j * (-1) ** m / sqrt(2)
            return A

        def real_w3j(l1, l2, l3):
            wc = _w3j_complex(l1, l2, l3).astype(complex)
            wr = np.einsum('abc,ma,nb,oc->mno', wc, _A(l1).conj(), _A(l2).conj(), _A(l3).conj())
            i = int(np.argmax(np.abs(wr)))
            ph = wr.flat[i] / abs(wr.flat[i])
            wr = wr / ph
            assert np.abs(wr.imag).max() < 1e-10
            return np.real(wr).astype(np.float32)
        _W3J = {}
        for _mo, _lo in RS:
            for _mi, _li in RS:
                for _lf in range(abs(_lo - _li), _lo + _li + 1):
                    if (_lo, _lf, _li) not in _W3J:
                        _W3J[_lo, _lf, _li] = jnp.asarray(real_w3j(_lo, _lf, _li))
        _NORM = []
        for _mo, _lo in RS:
            _num = sum((mi * (2 * min(_lo, li) + 1) for mi, li in RS))
            _NORM.append(sqrt(4.0 * pi) * sqrt(2.0 * _lo + 1.0) / sqrt(_num))
        _F_OFFS = [0] + list(np.cumsum([mi * (2 * li + 1) for mi, li in RS]))

        def spherical_harmonics(rel_vec):
            r = rel_vec / jnp.linalg.norm(rel_vec, axis=-1, keepdims=True)
            x, y, z = (r[:, 0], r[:, 1], r[:, 2])
            y0 = jnp.full_like(x, 0.5 / sqrt(pi))[:, None]
            c1 = sqrt(3.0 / (4.0 * pi))
            y1 = c1 * jnp.stack([y, z, x], axis=-1)
            c2a = 0.5 * sqrt(15.0 / pi)
            c2b = 0.25 * sqrt(5.0 / pi)
            c2c = 0.25 * sqrt(15.0 / pi)
            y2 = jnp.stack([c2a * x * y, c2a * y * z, c2b * (3.0 * z * z - 1.0), c2a * x * z, c2c * (x * x - y * y)], axis=-1)
            return jnp.concatenate([y0, y1, y2], axis=-1)
        src, dst = (edge_index[0], edge_index[1])
        R = jax.nn.relu(abs_distances[:, None] @ w1 + b1) @ w2 + b2
        Y = spherical_harmonics(rel_vec)
        Fj = features[src]
        E = Fj.shape[0]
        msg_blocks = []
        r_off = 0
        for i, (mo, lo) in enumerate(RS):
            acc = jnp.zeros((E, mo, 2 * lo + 1), dtype=features.dtype)
            for j, (mi, li) in enumerate(RS):
                n_lf = 2 * min(lo, li) + 1
                sz = mo * mi * n_lf
                Rb = R[:, r_off:r_off + sz].reshape(E, mo, mi, n_lf)
                r_off += sz
                Fb = Fj[:, _F_OFFS[j]:_F_OFFS[j + 1]].reshape(E, mi, 2 * li + 1)
                for k, lf in enumerate(range(abs(lo - li), lo + li + 1)):
                    C = _W3J[lo, lf, li]
                    Yf = Y[:, lf * lf:(lf + 1) * (lf + 1)]
                    acc = acc + _NORM[i] * jnp.einsum('euv,ef,evi,ofi->euo', Rb[..., k], Yf, Fb, C)
            msg_blocks.append(acc.reshape(E, -1))
        msg = jnp.concatenate(msg_blocks, axis=-1)
        out = jnp.zeros((features.shape[0], msg.shape[1]), dtype=features.dtype)
        out = out.at[dst].add(msg)
        return out
    edge_index = jnp.stack([src, dst])
    x = _layernorm(x + _L0_gnn_ref(x, edge_index, edge_attr_4, L0_gnn_W1, L0_gnn_b1, L0_gnn_W2, L0_gnn_b2, L0_gnn_W3, L0_gnn_b3, L0_gnn_W4, L0_gnn_b4), axis=-1)
    x = _layernorm(x + _L1_gnn_ref(x, edge_weight, edge_attr_3, edge_index, L1_gnn_w1, L1_gnn_b1, L1_gnn_w2, L1_gnn_b2), axis=-1)
    return x

_drawn_inputs = setup_inputs


def setup_inputs(seed=0):
    import zlib

    import numpy as np

    out = dict(_drawn_inputs(seed))
    spreads = {'L1_gnn_b1': (0.0, 0.1), 'L1_gnn_b2': (0.0, 0.1)}
    factors = {'L0_gnn_W1': 2.773, 'L0_gnn_b1': 8.0}
    for name, (base, spread) in spreads.items():
        noise = np.random.default_rng([zlib.crc32(name.encode()), seed]).standard_normal(out[name].shape)
        drawn = base * np.exp(spread * noise) if base else spread * noise
        out[name] = jnp.asarray(drawn.astype(out[name].dtype))
    for name, factor in factors.items():
        out[name] = (out[name] * factor).astype(out[name].dtype)
    return out
```

```python
import concourse.bass as bass
from concourse import mybir
from contextlib import ExitStack
from math import factorial, pi, sqrt

FP32 = mybir.dt.float32
I32 = mybir.dt.int32
U32 = mybir.dt.uint32
ALU = mybir.AluOpType
ACT = mybir.ActivationFunctionType
AX = mybir.AxisListType

NODES, EDGES = 12500, 400000
D, H, H2 = 32, 64, 128
MUL, RH = 8, 64
P = 128
TILES = EDGES // P
GT = 5
GE = GT * P
GROUPS = TILES // GT
W = 64
U = 5
BLOCKS = GROUPS // U
NQ, NC = 125, 100
RQ = TILES // NQ
GQ = GROUPS // NQ
PADN = NODES + W
SPLIT = 3
EPS = 1e-5
assert TILES * P == EDGES and GROUPS * GT == TILES and BLOCKS * U == GROUPS and NQ * NC == NODES

N0 = sqrt(4 * pi) / sqrt(MUL * 2)
N1 = sqrt(4 * pi) * sqrt(3.0) / sqrt(MUL + MUL * 3)
Y0 = 0.5 / sqrt(pi)
C1 = sqrt(3.0 / (4.0 * pi))
C2A = 0.5 * sqrt(15.0 / pi)
A00 = N0 * Y0
A01 = N0 * C1 / sqrt(3.0)
A10 = N1 * C1 / sqrt(3.0)
A110 = N1 * Y0 / sqrt(3.0)
A111 = N1 * C1 / sqrt(6.0)
A2 = N1 * C2A / sqrt(10.0)


def spread(ap, axis, n):
    ap = ap.unsqueeze(axis)
    shape = list(ap.shape)
    shape[axis] = n
    return ap.broadcast_to(shape)


def turns(eng, lag):
    peeled = 2 if lag else 1
    for b in range(peeled):
        for k in range(U):
            yield b, k
    with eng.Fori(peeled, BLOCKS) as b:
        for k in range(U):
            yield b, k
    for k in range(lag):
        yield BLOCKS, k


def live(b, k, lag):
    return not isinstance(b, int) or 0 <= b * U + k - lag < GROUPS


def slot(k, lag):
    return (k - lag) % U


def wait_groups(eng, sem, sweep, count, per_group=1):
    if not isinstance(count, int) or count > 0:
        eng.wait_ge(sem, (sweep * GROUPS + count) * per_group)


def wait_slot(eng, sem, sweep, b, k, lag, dmas=1):
    rounds = b + (k - lag) // U + 1
    if not isinstance(rounds, int) or rounds > 0:
        eng.wait_ge(sem[slot(k, lag)], (sweep * BLOCKS + rounds) * (16 * dmas))


def build(nc, t, out):
    ctx = ExitStack()
    with ctx:
        def sb(c, name, shape, dt=FP32):
            return c.enter_context(nc.sbuf_tensor(name, shape, dt))

        def pb(c, name):
            return c.enter_context(nc.psum_tensor(name, [128, 512], FP32))

        def sem(name):
            return ctx.enter_context(nc.semaphore(name))

        a_table = nc.dram_tensor("a_table", [PADN, H], FP32, kind="Internal").ap()
        b_table = nc.dram_tensor("b_table", [NODES, H], FP32, kind="Internal").ap()
        x1_table = nc.dram_tensor("x1_table", [NODES, D], FP32, kind="Internal").ap()
        base_dram = nc.dram_tensor("base_dram", [1, GROUPS], FP32, kind="Internal").ap()
        span_dram = nc.dram_tensor("span_dram", [1, NQ], FP32, kind="Internal").ap()

        ident = sb(ctx, "ident", [P, P])
        iota_row = sb(ctx, "iota_row", [P, W])
        iota_col = sb(ctx, "iota_col", [P, 1])
        eps_col = sb(ctx, "eps_col", [P, 1])
        dst_rel = sb(ctx, "dst_rel", [P, TILES])
        src_f = sb(ctx, "src_f", [P, TILES])
        x_nodes = sb(ctx, "x_nodes", [NQ, NC * D])
        base_bc = sb(ctx, "base_bc", [P, GROUPS])
        base_col = sb(ctx, "base_col", [W, GROUPS])
        base_i = sb(ctx, "base_i", [1, GROUPS], I32)
        sweeps_i = sb(ctx, "sweeps_i", [P, 1], I32)
        moved = sb(ctx, "moved", [P, 1])
        w2_sb = sb(ctx, "w2_sb", [H, H2])
        w3_sb = sb(ctx, "w3_sb", [H2, H])
        w4_sb = sb(ctx, "w4_sb", [H + 1, D + 1])
        b2_col = sb(ctx, "b2_col", [H2, 1])
        b3_bc = sb(ctx, "b3_bc", [P, H])
        r_w1 = sb(ctx, "r_w1", [RH + 1, 1])
        r_b1 = sb(ctx, "r_b1", [RH + 1, 1])
        r_w2 = sb(ctx, "r_w2", [RH + 1, 384])
        idx = sb(ctx, "idx", [P, U, GT], U32)

        setup_ids = sem("setup_ids")
        loaded = sem("loaded")
        link_v = sem("link_v")
        pe_setup = sem("pe_setup")
        dve_setup = sem("dve_setup")
        memo = {"v": 0}

        def link(ins):
            memo["v"] += 1
            ins.then_inc(link_v, 1)
            nc.vector.wait_ge(link_v, memo["v"])

        setup = ExitStack()
        with setup:
            rows_i = sb(setup, "rows_i", [NQ, RQ * P], I32)
            rows_f = sb(setup, "rows_f", [NQ, RQ * P])
            rows2_i = sb(setup, "rows2_i", [NQ, RQ * P], I32)
            rows2_f = rows2_i[:, :].bitcast(FP32)
            ab = sb(setup, "ab", [NQ, 2, NC * H])
            x_t = sb(setup, "x_t", [D, 2, 4 * NQ])
            w1_top = sb(setup, "w1_top", [D, H])
            w1_ab = sb(setup, "w1_ab", [D, 2 * H])
            b1_bc = sb(setup, "b1_bc", [P, H])
            r_raw = sb(setup, "r_raw", [RH + 1, 384])
            zero = sb(setup, "zero", [W, H])
            gmin = sb(setup, "gmin", [NQ, GQ])
            gmax = sb(setup, "gmax", [NQ, GQ])
            span = sb(setup, "span", [NQ, 1])
            span_row = sb(setup, "span_row", [P, NQ])
            span_i = sb(setup, "span_i", [P, 1], I32)
            rtmp = sb(setup, "rtmp", [RH + 1, 64])
            iota_i = sb(setup, "iota_i", [P, W], I32)
            iotc_i = sb(setup, "iotc_i", [P, 1], I32)
            ps = [pb(setup, f"ps_setup{i}") for i in range(4)]
            NB4 = NC // 4
            weights_in = sem("weights_in")
            x_in = sem("x_in")
            dst_in = sem("dst_in")
            src_in = sem("src_in")
            fills = sem("fills")
            base_out = sem("base_out")
            base_in = sem("base_in")
            tables_out = sem("tables_out")
            gmin_ready = sem("gmin_ready")
            span_ready = sem("span_ready")
            src_ready = sem("src_ready")
            xt_made = sem("xt_made")
            xt_copied = sem("xt_copied")
            ab_made = sem("ab_made")
            ab_copied = sem("ab_copied")
            idx_tr = sem("idx_tr")
            idx_copied = sem("idx_copied")
            n_w = 11

            with nc.Block() as block:
                @block.sync
                def _(sp):
                    sp.dma_start(rows_i[:, :], t["dst"].rearrange("(q n) -> q n", q=NQ)).then_inc(dst_in, 16)
                    sp.dma_start(x_nodes[:, :], t["x"].rearrange("(q c) d -> q (c d)", q=NQ)).then_inc(x_in, 16)
                    sp.wait_ge(fills, 8)
                    for dst, src in (
                        (w1_top[:, :], t["L0_gnn_W1"][0:D, :]),
                        (w1_ab[:, H:2 * H], t["L0_gnn_W1"][D:2 * D, :]),
                        (w2_sb[:, :], t["L0_gnn_W2"]),
                        (w3_sb[:, :], t["L0_gnn_W3"]),
                        (w4_sb[0:H, 0:D], t["L0_gnn_W4"]),
                        (w4_sb[H:H + 1, 0:D], t["L0_gnn_b4"].rearrange("(a n) -> a n", a=1)),
                        (b2_col[:, :], t["L0_gnn_b2"].rearrange("(n a) -> n a", a=1)),
                        (r_w1[0:RH, :], t["L1_gnn_w1"].rearrange("a n -> n a")),
                        (r_b1[0:RH, :], t["L1_gnn_b1"].rearrange("(n a) -> n a", a=1)),
                        (r_raw[0:RH, :], t["L1_gnn_w2"]),
                        (r_raw[RH:RH + 1, :], t["L1_gnn_b2"].rearrange("(a n) -> a n", a=1)),
                    ):
                        sp.dma_start(dst, src).then_inc(weights_in, 16)
                    sp.dma_start(rows2_i[:, :], t["src"].rearrange("(q n) -> q n", q=NQ)).then_inc(src_in, 16)
                    sp.wait_ge(gmin_ready, 1)
                    sp.wait_ge(span_ready, 1)
                    sp.dma_start(base_dram.rearrange("a (q k) -> (a q) k", q=NQ), gmin[:, :]).then_inc(base_out, 16)
                    sp.dma_start(span_dram.rearrange("a (q k) -> (a q) k", q=NQ), span[:, :]).then_inc(base_out, 16)
                    sp.wait_ge(base_out, 32)
                    sp.dma_start(base_bc[:, :], base_dram.broadcast_to([P, GROUPS])).then_inc(base_in, 16)
                    sp.dma_start(span_row[:, :], span_dram.broadcast_to([P, NQ])).then_inc(base_in, 16)
                    sp.wait_ge(ab_copied, NB4)
                    sp.dma_start(a_table[0:NODES, :].rearrange("(q c) h -> q (c h)", q=NQ), ab[:, 0, :]).then_inc(tables_out, 16)
                    sp.dma_start(b_table.rearrange("(q c) h -> q (c h)", q=NQ), ab[:, 1, :]).then_inc(tables_out, 16)
                    sp.dma_start(a_table[NODES:PADN, :], zero[:, :]).then_inc(tables_out, 16)
                    sp.wait_ge(tables_out, 48)

                @block.gpsimd
                def _(pool):
                    nc.gpsimd.memset(ident[:, :], 0.0).then_inc(setup_ids, 1)
                    nc.gpsimd.iota(iota_i[:, :], pattern=[[1, W]], base=0, channel_multiplier=0).then_inc(setup_ids, 1)
                    nc.gpsimd.iota(iotc_i[:, :], pattern=[[0, 1]], base=0, channel_multiplier=1).then_inc(setup_ids, 1)
                    pool.wait_ge(setup_ids, 3)
                    nc.gpsimd.affine_select(out=ident[:, :], in_=ident[:, :], compare_op=ALU.not_equal, fill=1.0,
                                            base=0, pattern=[[-1, P]], channel_multiplier=1).then_inc(setup_ids, 1)

                @block.scalar
                def _(act):
                    act.dma_start(b1_bc[:, :], spread(t["L0_gnn_b1"], 0, P)).then_inc(loaded, 16)
                    act.dma_start(b3_bc[:, :], spread(t["L0_gnn_b3"], 0, P)).then_inc(loaded, 16)
                    act.wait_ge(src_in, 16)
                    nc.scalar.activation(rows2_f, rows2_i[:, :], ACT.Copy).then_inc(src_ready, 1)
                    for b in range(NB4):
                        act.wait_ge(xt_made, b + 1)
                        if b >= 2:
                            act.wait_ge(ab_made, b - 1)
                        nc.scalar.copy(x_t[:, b % 2, :], ps[b % 2][0:D, 0:4 * NQ]).then_inc(xt_copied, 1)

                @block.vector
                def _(dve):
                    nc.vector.memset(w4_sb[:, :], 0.0).then_inc(link_v, 1)
                    memo["v"] += 1
                    dve.wait_ge(link_v, memo["v"])
                    nc.vector.memset(w4_sb[H:H + 1, D:D + 1], 1.0).then_inc(fills, 4)
                    nc.vector.memset(r_w1[:, :], 0.0).then_inc(fills, 1)
                    nc.vector.memset(r_b1[:, :], 1.0).then_inc(fills, 1)
                    nc.vector.memset(zero[:, :], 0.0).then_inc(fills, 1)
                    nc.vector.memset(eps_col[:, :], EPS).then_inc(fills, 1)
                    dve.wait_ge(setup_ids, 3)
                    nc.vector.tensor_copy(iota_row[:, :], iota_i[:, :])
                    link(nc.vector.tensor_copy(iota_col[:, :], iotc_i[:, :]))
                    dve.wait_ge(dst_in, 16)
                    link(nc.vector.tensor_copy(rows_f[:, :], rows_i[:, :]))
                    groups = rows_f[:, :].rearrange("q (k e) -> q k e", k=GQ)
                    nc.vector.tensor_reduce(gmin[:, :], groups, AX.X, ALU.min).then_inc(gmin_ready, 1)
                    link(nc.vector.tensor_reduce(gmax[:, :], groups, AX.X, ALU.max))
                    dve.wait_ge(gmin_ready, 1)
                    link(nc.vector.tensor_tensor(gmax[:, :], gmax[:, :], gmin[:, :], ALU.subtract))
                    nc.vector.tensor_reduce(span[:, :], gmax[:, :], AX.X, ALU.max).then_inc(span_ready, 1)
                    dve.wait_ge(weights_in, 16 * n_w)
                    nc.vector.tensor_tensor(w1_ab[:, 0:H], w1_top[:, :], w1_ab[:, H:2 * H], ALU.subtract).then_inc(dve_setup, 1)
                    mix = r_w2[:, 0:256].rearrange("h (x u s v) -> h x u s v", x=2, u=8, s=2)
                    vec = r_w2[:, 256:384].rearrange("h (u t v) -> h u t v", u=8, t=2)
                    k3 = r_raw[:, 192:384].rearrange("h (u v k) -> h u v k", u=8, v=8)

                    def flat(g):
                        return r_raw[:, 64 * g:64 * g + 64].rearrange("h (u v) -> h u v", u=8)

                    rt = rtmp[:, :].rearrange("h (u v) -> h u v", u=8)
                    link(nc.vector.tensor_scalar(rt, k3[:, :, :, 2], -A2 / 3.0, None, ALU.mult))
                    nc.vector.tensor_scalar(mix[:, 0, :, 0, :], flat(2), A10, None, ALU.mult)
                    nc.vector.tensor_scalar(mix[:, 0, :, 1, :], k3[:, :, :, 2], A2, None, ALU.mult)
                    nc.vector.tensor_scalar(mix[:, 1, :, 0, :], flat(0), A00, None, ALU.mult)
                    nc.vector.tensor_scalar(mix[:, 1, :, 1, :], flat(1), A01, None, ALU.mult)
                    nc.vector.scalar_tensor_tensor(out=vec[:, :, 0, :], in0=k3[:, :, :, 0], scalar=A110, in1=rt,
                                                   op0=ALU.mult, op1=ALU.add)
                    link(nc.vector.tensor_scalar(vec[:, :, 1, :], k3[:, :, :, 1], A111, None, ALU.mult))
                    dve.wait_ge(base_in, 32)
                    link(nc.vector.tensor_copy(base_i[:, :], base_bc[0:1, :]))
                    nc.vector.tensor_scalar(base_col[:, :], base_bc[0:W, :], iota_col[0:W, :], None, ALU.add)
                    link(nc.vector.tensor_reduce(span_row[:, 0:1], span_row[:, :], AX.X, ALU.max))
                    link(nc.vector.tensor_copy(span_i[:, :], span_row[:, 0:1]))
                    link(nc.vector.tensor_scalar(span_i[:, :], span_i[:, :], 6, None, ALU.logical_shift_right))
                    link(nc.vector.tensor_scalar(sweeps_i[:, :], span_i[:, :], 1, None, ALU.add))
                    link(nc.vector.tensor_scalar(moved[:, :], sweeps_i[:, :], float(W), None, ALU.mult))
                    dve.wait_ge(loaded, 32)
                    bias4 = spread(b1_bc[0:NQ, :], 1, 4)
                    for b in range(NB4):
                        dve.wait_ge(ab_made, b + 1)
                        pv = ps[2 + b % 2][0:NQ, :].rearrange("q (c z h) -> q c z h", c=4, z=2)
                        av = ab[:, :, b * 4 * H:(b + 1) * 4 * H].rearrange("q z (c h) -> q z c h", c=4)
                        nc.vector.tensor_tensor(av[:, 0], pv[:, :, 0, :], bias4, ALU.add)
                        nc.vector.tensor_copy(av[:, 1], pv[:, :, 1, :]).then_inc(ab_copied, 1)
                    for b in range(2 * 7):
                        n = min(4, RQ - 4 * (b % 7))
                        dve.wait_ge(idx_tr, b + 1)
                        target = (dst_rel, src_f)[b // 7][:, :].rearrange("p (q k) -> p k q", k=RQ)
                        nc.vector.tensor_copy(target[:, 4 * (b % 7):4 * (b % 7) + n, :],
                                              ps[b % 2][:, 0:n * NQ].rearrange("p (k q) -> p k q", k=n)).then_inc(idx_copied, 1)
                    dve.wait_ge(idx_copied, 14)
                    rel = dst_rel[:, :].rearrange("p (g j) -> p g j", j=GT)
                    link(nc.vector.tensor_tensor(rel, rel, spread(base_bc[:, :], 2, GT),
                                                 ALU.subtract))

                @block.tensor
                def _(pe):
                    pe.wait_ge(setup_ids, 4)
                    pe.wait_ge(x_in, 16)
                    pe.wait_ge(dve_setup, 1)

                    def columns(b):
                        pe.wait_ge(xt_copied, b + 1)
                        if b >= 2:
                            pe.wait_ge(ab_copied, b - 1)
                        for j in range(4):
                            last = nc.tensor.matmul(ps[2 + b % 2][0:NQ, j * 2 * H:(j + 1) * 2 * H],
                                                    x_t[:, b % 2, j * NQ:(j + 1) * NQ], w1_ab[:, :], start=True, stop=True)
                        last.then_inc(ab_made, 1)

                    for b in range(NB4):
                        if b >= 2:
                            pe.wait_ge(xt_copied, b - 1)
                        for j in range(4):
                            c = 4 * b + j
                            last = nc.tensor.transpose(ps[b % 2][0:D, j * NQ:(j + 1) * NQ],
                                                       x_nodes[:, c * D:(c + 1) * D], ident[0:NQ, 0:NQ])
                        last.then_inc(xt_made, 1)
                        if b >= 1:
                            columns(b - 1)
                    columns(NB4 - 1)
                    pe.wait_ge(gmin_ready, 1)
                    pe.wait_ge(src_ready, 1)
                    pe.wait_ge(xt_copied, NB4)
                    for b in range(2 * 7):
                        rows = (rows_f[:, :], rows2_f)[b // 7]
                        if b >= 2:
                            pe.wait_ge(idx_copied, b - 1)
                        for j in range(min(4, RQ - 4 * (b % 7))):
                            k = 4 * (b % 7) + j
                            last = nc.tensor.transpose(ps[b % 2][:, j * NQ:(j + 1) * NQ], rows[:, k * P:(k + 1) * P],
                                                       ident[0:NQ, 0:NQ])
                        last.then_inc(idx_tr, 1)

        acc = sb(ctx, "acc", [H + 1, PADN])

        gathers_begun = sem("gathers_begun")

        def move_windows(dve, swept):
            nc.vector.tensor_scalar(dst_rel[:, :], dst_rel[:, :], float(-W), None, ALU.add)
            nc.vector.tensor_scalar(base_col[:, :], base_col[:, :], float(W), None, ALU.add)
            nc.vector.tensor_scalar(base_i[:, :], base_i[:, :], W, NODES, ALU.add, ALU.min).then_inc(swept, 1)

        l0 = ExitStack()
        with l0:
            dst_t = sb(l0, "dst_t", [W, U, GE], I32)
            a_win = sb(l0, "a_win", [W, U, H])
            b_rows = sb(l0, "b_rows", [P, U, GT, H])
            pick_t = sb(l0, "pick_t", [W, U, GE])
            pick = sb(l0, "pick", [P, U, GT, W])
            h1 = sb(l0, "h1", [H, U, GE])
            h2 = sb(l0, "h2", [H2, U, GE])
            h3_raw = sb(l0, "h3_raw", [P, U, GT * H])
            h3 = sb(l0, "h3", [P, U, GT, H + 1])
            ps_h1 = [pb(l0, "ps_h1a"), pb(l0, "ps_h1b")]
            ps_h2 = [pb(l0, "ps_h2a"), pb(l0, "ps_h2b")]
            ps_h3 = pb(l0, "ps_h3")
            ps_sum = pb(l0, "ps_sum0")
            dst_t_in = [sem(f"dst_t_in{u}") for u in range(U)]
            a_win_in = [sem(f"a_win_in{u}") for u in range(U)]
            b_rows_in = [sem(f"b_rows_in{u}") for u in range(U)]
            idx_ready = sem("idx_ready")
            pick_t_made = sem("pick_t_made")
            pick_made = sem("pick_made")
            h1_made = sem("h1_made")
            h1_relu = sem("h1_relu")
            h2_made = sem("h2_made")
            h2_relu = sem("h2_relu")
            h3_made = sem("h3_made")
            h3_biased = sem("h3_biased")
            h3_relu = sem("h3_relu")
            sum_made = sem("sum_made")
            sum_added = sem("sum_added")
            swept = sem("swept")
            cleared = sem("cleared")
            halves = ((0, SPLIT), (SPLIT, GT))

            with nc.Block() as block:
                @block.sync
                def _(sp):
                    dst_rows = t["dst"].unsqueeze(0)
                    sweeps = sp.value_load(sweeps_i[0:1, 0:1], min_val=1, max_val=256)
                    with sp.Fori(0, sweeps) as s:
                        sp.wait_ge(swept, s + 1)
                        for b, k in turns(sp, 0):
                            g = b * U + k
                            wait_groups(sp, pick_t_made, s, g - U + 1)
                            sp.dma_start(dst_t[:, k, :], dst_rows[:, bass.ds(g * GE, GE)].broadcast_to([W, GE]))\
                                .then_inc(dst_t_in[k], 16)
                            wait_groups(sp, h1_made, s, g - U + 1)
                            base = sp.value_load(base_i[0:1, bass.ds(g, 1)], min_val=0, max_val=NODES)
                            sp.dma_start(a_win[:, k, :], a_table[bass.ds(base, W), :]).then_inc(a_win_in[k], 16)

                @block.gpsimd
                def _(pool):
                    sweeps = pool.value_load(sweeps_i[0:1, 0:1], min_val=1, max_val=256)
                    with pool.Fori(0, sweeps) as s:
                        pool.wait_ge(swept, s + 1)
                        for b, k in turns(pool, 0):
                            g = b * U + k
                            wait_groups(pool, idx_ready, s, g + 1)
                            wait_groups(pool, h1_made, s, g - U + 1)
                            pool.sem_inc(gathers_begun, 1)
                            for j in range(GT):
                                nc.gpsimd.indirect_dma_start(
                                    out=b_rows[:, k, j, :], out_offset=None, in_=b_table,
                                    in_offset=bass.IndirectOffsetOnAxis(ap=idx[:, k, j:j + 1], axis=0),
                                ).then_inc(b_rows_in[k], 16)

                @block.scalar
                def _(act):
                    sweeps = act.value_load(sweeps_i[0:1, 0:1], min_val=1, max_val=256)
                    with act.Fori(0, sweeps) as s:
                        act.wait_ge(swept, s + 1)
                        for b, k in turns(act, 4):
                            g = b * U + k
                            if live(b, k, 0):
                                wait_slot(act, b_rows_in, s, b - 1, k, 0, GT)
                                nc.scalar.activation(idx[:, k, :], src_f[:, bass.ds(g * GT, GT)], ACT.Copy).then_inc(idx_ready, 1)
                            if live(b, k, 2):
                                z = slot(k, 2)
                                wait_groups(act, h1_made, s, g - 2 + 1)
                                wait_groups(act, h2_made, s, g - 2 - U + 1)
                                for (lo, hi), ps in zip(halves, ps_h1):
                                    last = nc.scalar.activation(h1[:, z, lo * P:hi * P], ps[0:H, 0:(hi - lo) * P], ACT.Relu)
                                last.then_inc(h1_relu, 1)
                            if live(b, k, 3):
                                z = slot(k, 3)
                                wait_groups(act, h2_made, s, g - 3 + 1)
                                wait_groups(act, h3_made, s, g - 3 - U + 1)
                                for (lo, hi), ps in zip(halves, ps_h2):
                                    last = nc.scalar.activation(h2[:, z, lo * P:hi * P], ps[:, 0:(hi - lo) * P], ACT.Relu,
                                                                bias=b2_col[:, :])
                                last.then_inc(h2_relu, 1)
                            if live(b, k, 4):
                                z = slot(k, 4)
                                wait_groups(act, h3_biased, s, g - 4 + 1)
                                wait_groups(act, sum_made, s, g - 4 - U + 1)
                                nc.scalar.activation(h3[:, z, :, 0:H], h3_raw[:, z, :].rearrange("p (j h) -> p j h", j=GT),
                                                     ACT.Relu).then_inc(h3_relu, 1)

                @block.tensor
                def _(pe):
                    sweeps = pe.value_load(sweeps_i[0:1, 0:1], min_val=1, max_val=256)
                    with pe.Fori(0, sweeps) as s:
                        pe.wait_ge(swept, s + 1)
                        for b, k in turns(pe, 3):
                            g = b * U + k
                            if live(b, k, 0):
                                wait_groups(pe, pick_t_made, s, g + 1)
                                wait_slot(pe, a_win_in, s, b, k, 0)
                                wait_slot(pe, b_rows_in, s, b, k, 0, GT)
                                wait_groups(pe, h1_relu, s, g)
                                for (lo, hi), ps in zip(halves, ps_h1):
                                    for j in range(lo, hi):
                                        nc.tensor.matmul(ps[0:H, (j - lo) * P:(j - lo + 1) * P], b_rows[:, k, j, :],
                                                         ident[:, :], start=(j == lo), stop=False)
                                    last = nc.tensor.matmul(ps[0:H, 0:(hi - lo) * P], a_win[:, k, :], pick_t[:, k, lo * P:hi * P],
                                                            start=False, stop=True)
                                last.then_inc(h1_made, 1)
                            if live(b, k, 1):
                                z = slot(k, 1)
                                wait_groups(pe, h1_relu, s, g - 1 + 1)
                                wait_groups(pe, h2_relu, s, g - 1)
                                for (lo, hi), ps in zip(halves, ps_h2):
                                    last = nc.tensor.matmul(ps[:, 0:(hi - lo) * P], w2_sb[:, :], h1[:, z, lo * P:hi * P],
                                                            start=True, stop=True)
                                last.then_inc(h2_made, 1)
                            if live(b, k, 2):
                                z = slot(k, 2)
                                wait_groups(pe, h2_relu, s, g - 2 + 1)
                                wait_groups(pe, h3_biased, s, g - 2)
                                for j in range(GT):
                                    last = nc.tensor.matmul(ps_h3[:, j * H:(j + 1) * H], h2[:, z, j * P:(j + 1) * P], w3_sb[:, :],
                                                            start=True, stop=True)
                                last.then_inc(h3_made, 1)
                            if live(b, k, 3):
                                z = slot(k, 3)
                                wait_groups(pe, h3_relu, s, g - 3 + 1)
                                wait_groups(pe, pick_made, s, g - 3 + 1)
                                wait_groups(pe, sum_added, s, g - 3)
                                if isinstance(b, int) and b == 0:
                                    pe.wait_ge(cleared, 2)
                                for j in range(GT):
                                    last = nc.tensor.matmul(ps_sum[0:H + 1, 0:W], h3[:, z, j, :], pick[:, z, j, :],
                                                            start=(j == 0), stop=(j == GT - 1))
                                last.then_inc(sum_made, 1)

                @block.vector
                def _(dve):
                    nc.vector.memset(h3[:, :, :, H:H + 1], 1.0).then_inc(cleared, 1)
                    nc.vector.memset(acc[:, :], 0.0).then_inc(cleared, 1)
                    dve.wait_ge(cleared, 2)
                    dve.sem_inc(swept, 1)
                    sweeps = dve.value_load(sweeps_i[0:1, 0:1], min_val=1, max_val=256)
                    with dve.Fori(0, sweeps) as s:
                        dve.wait_ge(swept, s + 1)
                        for b, k in turns(dve, 4):
                            g = b * U + k
                            if live(b, k, 0):
                                wait_slot(dve, dst_t_in, s, b, k, 0)
                                wait_groups(dve, h1_made, s, g - U + 1)
                                nc.vector.tensor_scalar(pick_t[:, k, :], dst_t[:, k, :], base_col[:, bass.ds(g, 1)], None,
                                                        ALU.is_equal).then_inc(pick_t_made, 1)
                                wait_groups(dve, sum_made, s, g - U + 1)
                                nc.vector.tensor_tensor(pick[:, k], spread(dst_rel[:, bass.ds(g * GT, GT)], 2, W),
                                                        spread(iota_row[:, :], 1, GT), ALU.is_equal).then_inc(pick_made, 1)
                            if live(b, k, 3):
                                z = slot(k, 3)
                                wait_groups(dve, h3_made, s, g - 3 + 1)
                                wait_groups(dve, h3_relu, s, g - 3 - U + 1)
                                nc.vector.tensor_tensor(h3_raw[:, z, :].rearrange("p (j h) -> p j h", j=GT),
                                                        ps_h3[:, 0:GT * H].rearrange("p (j h) -> p j h", j=GT),
                                                        spread(b3_bc[:, :], 1, GT), ALU.add).then_inc(h3_biased, 1)
                            if live(b, k, 4):
                                base = dve.value_load(base_i[0:1, bass.ds(g - 4, 1)], min_val=0, max_val=NODES)
                                wait_groups(dve, sum_made, s, g - 4 + 1)
                                wait_groups(dve, sum_added, s, g - 4)
                                nc.vector.tensor_tensor(acc[:, bass.ds(base, W)], acc[:, bass.ds(base, W)],
                                                        ps_sum[0:H + 1, 0:W], ALU.add).then_inc(sum_added, 1)
                        wait_groups(dve, sum_added, s, GROUPS)
                        move_windows(dve, swept)

        def node_step(last):
            step = ExitStack()
            n_out = D if last else D + 1
            tag = "1" if last else "0"
            chunks = [(c, min(15, NC - c)) for c in range(0, NC, 15)]
            with step:
                y = sb(step, "y" + tag, [NQ, NC, n_out])
                sq = sb(step, "sq" + tag, [NQ, NC, D])
                stat = sb(step, "stat" + tag, [NQ, 4, NC])
                ps = [pb(step, f"ps_node{tag}{i}") for i in range(2)]
                out_made = sem("out_made" + tag)
                out_copied = sem("out_copied" + tag)
                spread_made = sem("spread_made" + tag)
                root_made = sem("root_made" + tag)
                normed = sem("normed" + tag)
                stored = sem("stored" + tag)
                with nc.Block() as block:
                    @block.tensor
                    def _(pe):
                        for n, (c0, cn) in enumerate(chunks):
                            if n >= 2:
                                pe.wait_ge(out_copied, n - 1)
                            for c in range(c0, c0 + cn):
                                lo = (c - c0) * n_out
                                if last:
                                    mm = nc.tensor.matmul(ps[n % 2][0:NQ, lo:lo + n_out], acc[0:D, c:NODES:NC],
                                                          ident[0:D, 0:D], start=True, stop=True)
                                else:
                                    mm = nc.tensor.matmul(ps[n % 2][0:NQ, lo:lo + n_out], acc[:, c:NODES:NC],
                                                          w4_sb[:, :], start=True, stop=True)
                            mm.then_inc(out_made, 1)

                    @block.scalar
                    def _(act):
                        act.wait_ge(spread_made, 1)
                        nc.scalar.activation(stat[:, 2, :], stat[:, 1, :], ACT.Sqrt, bias=eps_col[0:NQ, :], scale=1.0 / D)\
                            .then_inc(root_made, 1)

                    @block.vector
                    def _(dve):
                        for n, (c0, cn) in enumerate(chunks):
                            dve.wait_ge(out_made, n + 1)
                            nc.vector.tensor_copy(y[:, c0:c0 + cn, :], ps[n % 2][0:NQ, 0:cn * n_out].rearrange("q (c d) -> q c d", c=cn))\
                                .then_inc(out_copied, 1)
                        dve.wait_ge(out_copied, len(chunks))
                        yd = y[:, :, 0:D]
                        xv = x_nodes[:, :].rearrange("q (c d) -> q c d", c=NC)
                        if not last:
                            link(nc.vector.tensor_scalar(stat[:, 0, :], y[:, :, D], 1.0, None, ALU.max))
                            link(nc.vector.reciprocal(stat[:, 3, :], stat[:, 0, :]))
                            link(nc.vector.tensor_tensor(yd, yd, spread(stat[:, 3, :], 2, D), ALU.mult))
                        link(nc.vector.tensor_tensor(yd, yd, xv, ALU.add))
                        link(nc.vector.tensor_reduce(stat[:, 0, :], yd, AX.X, ALU.add))
                        link(nc.vector.tensor_scalar(stat[:, 0, :], stat[:, 0, :], 1.0 / D, None, ALU.mult))
                        link(nc.vector.tensor_tensor(yd, yd, spread(stat[:, 0, :], 2, D), ALU.subtract))
                        link(nc.vector.tensor_tensor(sq[:, :, :], yd, yd, ALU.mult))
                        nc.vector.tensor_reduce(stat[:, 1, :], sq[:, :, :], AX.X, ALU.add).then_inc(spread_made, 1)
                        dve.wait_ge(root_made, 1)
                        link(nc.vector.reciprocal(stat[:, 3, :], stat[:, 2, :]))
                        nc.vector.tensor_tensor(xv, yd, spread(stat[:, 3, :], 2, D), ALU.mult).then_inc(normed, 1)

                    @block.sync
                    def _(sp):
                        target = out if last else x1_table
                        sp.wait_ge(normed, 1)
                        sp.dma_start(target.rearrange("(q c) d -> q (c d)", q=NQ), x_nodes[:, :]).then_inc(stored, 16)
                        sp.wait_ge(stored, 16)

        node_step(False)

        unit = sb(ctx, "unit", [P, 3, TILES])
        prep = ExitStack()
        with prep:
            attr_rows = sb(prep, "attr_rows", [NQ, RQ, P, 3])
            norm = sb(prep, "norm", [P, TILES])
            part = sb(prep, "part", [P, TILES])
            ps = [pb(prep, f"ps_unit{i}") for i in range(2)]
            attr_in = sem("attr_in")
            axis_turned = sem("axis_turned")
            axis_copied = sem("axis_copied")
            squares_made = sem("squares_made")
            norm_made = sem("norm_made")
            cleared1 = sem("cleared1")
            axes = (1, 2, 0)
            turns_n = [(n, c, 4 * m, min(4, RQ - 4 * m)) for n, c in enumerate(axes) for m in range(7)]
            with nc.Block() as block:
                @block.sync
                def _(sp):
                    sp.dma_start(attr_rows[:, :, :, :].rearrange("q k p c -> q (k p c)"),
                                 t["edge_attr_3"].rearrange("(q n) c -> q (n c)", q=NQ)).then_inc(attr_in, 16)

                @block.tensor
                def _(pe):
                    pe.wait_ge(attr_in, 16)
                    for m, (n, c, k0, kn) in enumerate(turns_n):
                        if m >= 2:
                            pe.wait_ge(axis_copied, m - 1)
                        for k in range(k0, k0 + kn):
                            last = nc.tensor.transpose(ps[m % 2][:, (k - k0) * NQ:(k - k0 + 1) * NQ], attr_rows[:, k, :, c],
                                                       ident[0:NQ, 0:NQ])
                        last.then_inc(axis_turned, 1)

                @block.scalar
                def _(act):
                    act.wait_ge(squares_made, 1)
                    nc.scalar.activation(norm[:, :], norm[:, :], ACT.Sqrt).then_inc(norm_made, 1)

                @block.vector
                def _(dve):
                    nc.vector.memset(acc[0:D, :], 0.0)
                    nc.vector.tensor_scalar(dst_rel[:, :], dst_rel[:, :], moved[:, 0:1], None, ALU.add)
                    nc.vector.tensor_copy(base_i[:, :], base_bc[0:1, :])
                    for m, (n, c, k0, kn) in enumerate(turns_n):
                        dve.wait_ge(axis_turned, m + 1)
                        nc.vector.tensor_copy(unit[:, n, :].rearrange("p (q k) -> p k q", k=RQ)[:, k0:k0 + kn, :],
                                              ps[m % 2][:, 0:kn * NQ].rearrange("p (k q) -> p k q", k=kn)).then_inc(axis_copied, 1)
                    dve.wait_ge(axis_copied, len(turns_n))
                    nc.vector.tensor_tensor(norm[:, :], unit[:, 0, :], unit[:, 0, :], ALU.mult)
                    link(nc.vector.tensor_tensor(part[:, :], unit[:, 1, :], unit[:, 1, :], ALU.mult))
                    link(nc.vector.tensor_tensor(norm[:, :], norm[:, :], part[:, :], ALU.add))
                    link(nc.vector.tensor_tensor(part[:, :], unit[:, 2, :], unit[:, 2, :], ALU.mult))
                    nc.vector.tensor_tensor(norm[:, :], norm[:, :], part[:, :], ALU.add).then_inc(squares_made, 1)
                    dve.wait_ge(norm_made, 1)
                    link(nc.vector.reciprocal(norm[:, :], norm[:, :]))
                    link(nc.vector.tensor_tensor(unit[:, :, :], unit[:, :, :], spread(norm[:, :], 1, 3), ALU.mult))

        l1 = ExitStack()
        with l1:
            hid = sb(l1, "hid", [RH + 1, U, GE])
            f_rows = sb(l1, "f_rows", [P, U, GT, D])
            pick = sb(l1, "pick1", [P, U, GT, W])
            n5 = sb(l1, "n5", [P, U, GT, 5])
            f5 = sb(l1, "f5", [P, U, GT, 5, MUL])
            mix_in = sb(l1, "mix_in", [P, U, GT, 2, MUL])
            vec_in = sb(l1, "vec_in", [P, U, GT, 3, 2, MUL])
            dots = sb(l1, "dots", [P, GT, MUL, 3])
            cross = sb(l1, "cross", [P, 2, GT, 3, MUL])
            prods = sb(l1, "prods", [P, GT, 40, 16])
            sums = sb(l1, "sums", [P, U, GT, 40])
            along = sb(l1, "along", [P, GT, MUL, 3])
            ps_r = [pb(l1, f"ps_r{j}") for j in range(GT)]
            ps_sum = pb(l1, "ps_sum1")
            weight_in = [sem(f"weight_in{u}") for u in range(U)]
            f_rows_in = [sem(f"f_rows_in{u}") for u in range(U)]
            idx_ready = sem("idx_ready1")
            hid_made = sem("hid_made")
            n5_made = sem("n5_made")
            f_copied = sem("f_copied")
            r_made = sem("r_made")
            r_used = sem("r_used")
            pick_made = sem("pick_made1")
            dots_made = sem("dots_made")
            cross_made = sem("cross_made")
            mix_made = sem("mix_made")
            vec_made = sem("vec_made")
            sums_made = sem("sums_made")
            along_made = sem("along_made")
            msg_made = sem("msg_made")
            sum_made = sem("sum_made1")
            sum_added = sem("sum_added1")
            swept = sem("swept1")

            def wait_tile(eng, sem, sweep, g, j):
                if not isinstance(g, int) or g >= 0:
                    eng.wait_ge(sem, (sweep * GROUPS + g) * GT + (j + 1))

            with nc.Block() as block:
                @block.sync
                def _(sp):
                    weights = t["edge_weight"].unsqueeze(0)
                    sweeps = sp.value_load(sweeps_i[0:1, 0:1], min_val=1, max_val=256)
                    with sp.Fori(0, sweeps) as s:
                        sp.wait_ge(swept, s + 1)
                        for b, k in turns(sp, 0):
                            g = b * U + k
                            wait_tile(sp, r_made, s, g - U, GT - 1)
                            sp.dma_start(hid[:, k, :], weights[:, bass.ds(g * GE, GE)].broadcast_to([RH + 1, GE]))\
                                .then_inc(weight_in[k], 16)

                @block.gpsimd
                def _(pool):
                    sweeps = pool.value_load(sweeps_i[0:1, 0:1], min_val=1, max_val=256)
                    with pool.Fori(0, sweeps) as s:
                        pool.wait_ge(swept, s + 1)
                        for b, k in turns(pool, 0):
                            g = b * U + k
                            wait_groups(pool, idx_ready, s, g + 1)
                            wait_groups(pool, f_copied, s, g - U + 1)
                            pool.sem_inc(gathers_begun, 1)
                            for j in range(GT):
                                nc.gpsimd.indirect_dma_start(
                                    out=f_rows[:, k, j, :], out_offset=None, in_=x1_table,
                                    in_offset=bass.IndirectOffsetOnAxis(ap=idx[:, k, j:j + 1], axis=0),
                                ).then_inc(f_rows_in[k], 16)

                @block.scalar
                def _(act):
                    sweeps = act.value_load(sweeps_i[0:1, 0:1], min_val=1, max_val=256)
                    with act.Fori(0, sweeps) as s:
                        act.wait_ge(swept, s + 1)
                        for b, k in turns(act, 2):
                            g = b * U + k
                            if live(b, k, 0):
                                wait_slot(act, f_rows_in, s, b - 1, k, 0, GT)
                                nc.scalar.activation(idx[:, k, :], src_f[:, bass.ds(g * GT, GT)], ACT.Copy).then_inc(idx_ready, 1)
                                wait_slot(act, weight_in, s, b, k, 0)
                                nc.scalar.activation(hid[:, k, :], hid[:, k, :], ACT.Relu, bias=r_b1[:, :], scale=r_w1[:, :])\
                                    .then_inc(hid_made, 1)
                                wait_groups(act, msg_made, s, g - U + 1)
                                nv = unit[:, :, bass.ds(g * GT, GT)].rearrange("p o j -> p j o")
                                nc.scalar.copy(n5[:, k, :, 0:3], nv)
                                nc.scalar.copy(n5[:, k, :, 3:5], nv[:, :, 0:2]).then_inc(n5_made, 1)
                            if live(b, k, 2):
                                z = slot(k, 2)
                                wait_slot(act, f_rows_in, s, b, k, 2, GT)
                                wait_groups(act, msg_made, s, g - 2 - U + 1)
                                f1 = f_rows[:, z, :, MUL:D].rearrange("p j (v o) -> p j o v", v=MUL)
                                nc.scalar.copy(mix_in[:, z, :, 0, :], f_rows[:, z, :, 0:MUL])
                                nc.scalar.copy(f5[:, z, :, 0:3, :], f1)
                                nc.scalar.copy(f5[:, z, :, 3:5, :], f1[:, :, 0:2, :])
                                nc.scalar.copy(vec_in[:, z, :, :, 0, :], f1).then_inc(f_copied, 1)

                @block.tensor
                def _(pe):
                    sweeps = pe.value_load(sweeps_i[0:1, 0:1], min_val=1, max_val=256)
                    with pe.Fori(0, sweeps) as s:
                        pe.wait_ge(swept, s + 1)
                        for b, k in turns(pe, 1):
                            g = b * U + k
                            if live(b, k, 0):
                                wait_groups(pe, hid_made, s, g + 1)
                                for j in range(GT):
                                    wait_tile(pe, r_used, s, g - 1, j)
                                    nc.tensor.matmul(ps_r[j][:, 0:384], hid[:, k, j * P:(j + 1) * P], r_w2[:, :],
                                                     start=True, stop=True).then_inc(r_made, 1)
                            if live(b, k, 1):
                                z = slot(k, 1)
                                wait_groups(pe, msg_made, s, g - 1 + 1)
                                wait_groups(pe, pick_made, s, g - 1 + 1)
                                wait_groups(pe, sum_added, s, g - 1)
                                for j in range(GT):
                                    last = nc.tensor.matmul(ps_sum[0:D, 0:W], sums[:, z, j, 8:40], pick[:, z, j, :],
                                                            start=(j == 0), stop=(j == GT - 1))
                                last.then_inc(sum_made, 1)

                @block.vector
                def _(dve):
                    dve.sem_inc(swept, 1)
                    sweeps = dve.value_load(sweeps_i[0:1, 0:1], min_val=1, max_val=256)
                    with dve.Fori(0, sweeps) as s:
                        dve.wait_ge(swept, s + 1)
                        for b, k in turns(dve, 1):
                            g = b * U + k
                            if live(b, k, 0):
                                wait_groups(dve, sum_made, s, g - U + 1)
                                nc.vector.tensor_tensor(pick[:, k], spread(dst_rel[:, bass.ds(g * GT, GT)], 2, W),
                                                        spread(iota_row[:, :], 1, GT), ALU.is_equal).then_inc(pick_made, 1)
                                wait_groups(dve, n5_made, s, g + 1)
                                wait_groups(dve, f_copied, s, g + 1)
                                nc.vector.tensor_tensor(dots[:, :, :, :], f5[:, k, :, 0:3, :].rearrange("p j o v -> p j v o"),
                                                        spread(n5[:, k, :, 0:3], 2, MUL), ALU.mult).then_inc(dots_made, 1)
                                nc.vector.tensor_tensor(cross[:, 0], f5[:, k, :, 2:5, :], spread(n5[:, k, :, 1:4], 3, MUL), ALU.mult)
                                nc.vector.tensor_tensor(cross[:, 1], f5[:, k, :, 1:4, :], spread(n5[:, k, :, 2:5], 3, MUL), ALU.mult)\
                                    .then_inc(cross_made, 1)
                                wait_groups(dve, dots_made, s, g + 1)
                                nc.vector.tensor_reduce(mix_in[:, k, :, 1, :], dots[:, :, :, :], AX.X, ALU.add).then_inc(mix_made, 1)
                                wait_groups(dve, cross_made, s, g + 1)
                                nc.vector.tensor_tensor(vec_in[:, k, :, :, 1, :], cross[:, 0], cross[:, 1], ALU.subtract).then_inc(vec_made, 1)
                            if live(b, k, 1):
                                base = dve.value_load(base_i[0:1, bass.ds(g - 1, 1)], min_val=0, max_val=NODES)
                                wait_groups(dve, sum_made, s, g - 1 + 1)
                                wait_groups(dve, sum_added, s, g - 1)
                                nc.vector.tensor_tensor(acc[0:D, bass.ds(base, W)], acc[0:D, bass.ds(base, W)],
                                                        ps_sum[0:D, 0:W], ALU.add).then_inc(sum_added, 1)
                            if live(b, k, 0):
                                wait_groups(dve, mix_made, s, g + 1)
                                wait_groups(dve, vec_made, s, g + 1)
                                for j in range(GT):
                                    wait_tile(dve, r_made, s, g, j)
                                    nc.vector.tensor_tensor(
                                        prods[:, j, 0:16, :], ps_r[j][:, 0:256].rearrange("p (r s) -> p r s", r=16),
                                        spread(mix_in[:, k, j].rearrange("p s v -> p (s v)"), 1, 16), ALU.mult)
                                    nc.vector.tensor_tensor(
                                        prods[:, j, 16:40, :].rearrange("p (u o) s -> p u o s", u=MUL),
                                        spread(ps_r[j][:, 256:384].rearrange("p (u s) -> p u s", u=MUL), 2, 3),
                                        spread(vec_in[:, k, j].rearrange("p o t v -> p o (t v)"), 1, MUL), ALU.mult)\
                                        .then_inc(r_used, 1)
                                wait_tile(dve, r_used, s, g, GT - 1)
                                nc.vector.tensor_reduce(sums[:, k].rearrange("p j r -> p (j r)"),
                                                        prods[:, :, :, :].rearrange("p j r s -> p (j r) s"), AX.X, ALU.add)\
                                    .then_inc(sums_made, 1)
                                wait_groups(dve, sums_made, s, g + 1)
                                nc.vector.tensor_tensor(along[:, :, :, :], spread(sums[:, k, :, 0:MUL], 3, 3),
                                                        spread(n5[:, k, :, 0:3], 2, MUL), ALU.mult).then_inc(along_made, 1)
                                wait_groups(dve, along_made, s, g + 1)
                                vec = sums[:, k, :, 16:40].rearrange("p j (u o) -> p j u o", u=MUL)
                                nc.vector.tensor_tensor(vec, vec, along[:, :, :, :], ALU.add).then_inc(msg_made, 1)
                        wait_groups(dve, sum_added, s, GROUPS)
                        move_windows(dve, swept)

        node_step(True)


_INS = ["x", "src", "dst", "edge_attr_3", "edge_weight", "L0_gnn_W1", "L0_gnn_b1", "L0_gnn_W2", "L0_gnn_b2",
        "L0_gnn_W3", "L0_gnn_b3", "L0_gnn_W4", "L0_gnn_b4", "L1_gnn_w1", "L1_gnn_b1", "L1_gnn_w2", "L1_gnn_b2"]


def kernel(**inputs):
    import numpy as _np
    import concourse.bacc as _bacc
    from concourse import mybir as _mybir
    from concourse.bass_utils import run_bass_kernel_spmd as _run

    nc = _bacc.Bacc("TRN2", target_bir_lowering=False, num_devices=1)
    arrays, tensors = {}, {}
    for name in _INS:
        a = _np.ascontiguousarray(inputs[name])
        arrays[f"in_{name}_dram"] = a
        tensors[name] = nc.dram_tensor(f"in_{name}_dram", a.shape, _mybir.dt.from_np(a.dtype), kind="ExternalInput").ap()
    out = nc.dram_tensor("out_dram", (NODES, D), FP32, kind="ExternalOutput").ap()
    build(nc, tensors, out)
    r = _run(nc, [arrays], core_ids=[0])
    return r.results[0]["out_dram"]
```

```python
import concourse.bass as bass
from concourse import mybir
from contextlib import ExitStack
from math import factorial, pi, sqrt

FP32 = mybir.dt.float32
I32 = mybir.dt.int32
U32 = mybir.dt.uint32
ALU = mybir.AluOpType
ACT = mybir.ActivationFunctionType
AX = mybir.AxisListType

NODES, EDGES = 12500, 400000
D, H, H2 = 32, 64, 128
MUL, RH = 8, 64
P = 128
TILES = EDGES // P
GT = 5
GE = GT * P
GROUPS = TILES // GT
W = 64
U = 5
BLOCKS = GROUPS // U
NQ, NC = 125, 100
RQ = TILES // NQ
GQ = GROUPS // NQ
PADN = NODES + W
SPLIT = 3
ROWS = 24
CH = (40 - ROWS) * 16 // P
TILE_LAG = 3
EPS = 1e-5
assert TILES * P == EDGES and GROUPS * GT == TILES and BLOCKS * U == GROUPS and NQ * NC == NODES

N0 = sqrt(4 * pi) / sqrt(MUL * 2)
N1 = sqrt(4 * pi) * sqrt(3.0) / sqrt(MUL + MUL * 3)
Y0 = 0.5 / sqrt(pi)
C1 = sqrt(3.0 / (4.0 * pi))
C2A = 0.5 * sqrt(15.0 / pi)
A00 = N0 * Y0
A01 = N0 * C1 / sqrt(3.0)
A10 = N1 * C1 / sqrt(3.0)
A110 = N1 * Y0 / sqrt(3.0)
A111 = N1 * C1 / sqrt(6.0)
A2 = N1 * C2A / sqrt(10.0)


def spread(ap, axis, n):
    ap = ap.unsqueeze(axis)
    shape = list(ap.shape)
    shape[axis] = n
    return ap.broadcast_to(shape)


def turns(eng, lag):
    peeled = 2 if lag else 1
    for b in range(peeled):
        for k in range(U):
            yield b, k
    with eng.Fori(peeled, BLOCKS) as b:
        for k in range(U):
            yield b, k
    for k in range(lag):
        yield BLOCKS, k


def live(b, k, lag):
    return not isinstance(b, int) or 0 <= b * U + k - lag < GROUPS


def slot(k, lag):
    return (k - lag) % U


def wait_groups(eng, sem, sweep, count, per_group=1):
    if not isinstance(count, int) or count > 0:
        eng.wait_ge(sem, (sweep * GROUPS + count) * per_group)


def wait_slot(eng, sem, sweep, b, k, lag, dmas=1):
    rounds = b + (k - lag) // U + 1
    if not isinstance(rounds, int) or rounds > 0:
        eng.wait_ge(sem[slot(k, lag)], (sweep * BLOCKS + rounds) * (16 * dmas))


def build(nc, t, out):
    ctx = ExitStack()
    with ctx:
        def sb(c, name, shape, dt=FP32):
            return c.enter_context(nc.sbuf_tensor(name, shape, dt))

        def pb(c, name):
            return c.enter_context(nc.psum_tensor(name, [128, 512], FP32))

        def sem(name):
            return ctx.enter_context(nc.semaphore(name))

        a_table = nc.dram_tensor("a_table", [PADN, H], FP32, kind="Internal").ap()
        b_table = nc.dram_tensor("b_table", [NODES, H], FP32, kind="Internal").ap()
        x1_table = nc.dram_tensor("x1_table", [NODES, D], FP32, kind="Internal").ap()
        base_dram = nc.dram_tensor("base_dram", [1, GROUPS], FP32, kind="Internal").ap()
        span_dram = nc.dram_tensor("span_dram", [1, NQ], FP32, kind="Internal").ap()

        ident = sb(ctx, "ident", [P, P])
        iota_row = sb(ctx, "iota_row", [P, W])
        iota_col = sb(ctx, "iota_col", [P, 1])
        eps_col = sb(ctx, "eps_col", [P, 1])
        one_col = sb(ctx, "one_col", [P, 1])
        dst_rel = sb(ctx, "dst_rel", [P, TILES])
        src_f = sb(ctx, "src_f", [P, TILES])
        x_nodes = sb(ctx, "x_nodes", [NQ, NC * D])
        base_bc = sb(ctx, "base_bc", [P, GROUPS])
        base_col = sb(ctx, "base_col", [W, GROUPS])
        base_i = sb(ctx, "base_i", [1, GROUPS], I32)
        sweeps_i = sb(ctx, "sweeps_i", [P, 1], I32)
        moved = sb(ctx, "moved", [P, 1])
        w2_sb = sb(ctx, "w2_sb", [H, H2])
        w3_sb = sb(ctx, "w3_sb", [H2, H])
        w4_sb = sb(ctx, "w4_sb", [H + 1, D + 1])
        b2_col = sb(ctx, "b2_col", [H2, 1])
        b3_bc = sb(ctx, "b3_bc", [P, H])
        r_w1 = sb(ctx, "r_w1", [RH + 1, 1])
        r_b1 = sb(ctx, "r_b1", [RH + 1, 1])
        r_w2 = sb(ctx, "r_w2", [P, 384])
        sum16 = sb(ctx, "sum16", [P, CH, D])
        idx = sb(ctx, "idx", [P, U, GT], U32)

        setup_ids = sem("setup_ids")
        sum16_step = sem("sum16_step")
        loaded = sem("loaded")
        link_v = sem("link_v")
        pe_setup = sem("pe_setup")
        dve_setup = sem("dve_setup")
        memo = {"v": 0}

        def link(ins):
            memo["v"] += 1
            ins.then_inc(link_v, 1)
            nc.vector.wait_ge(link_v, memo["v"])

        setup = ExitStack()
        with setup:
            rows_i = sb(setup, "rows_i", [NQ, RQ * P], I32)
            rows_f = sb(setup, "rows_f", [NQ, RQ * P])
            rows2_i = sb(setup, "rows2_i", [NQ, RQ * P], I32)
            rows2_f = rows2_i[:, :].bitcast(FP32)
            ab = sb(setup, "ab", [NQ, 2, NC * H])
            x_t = sb(setup, "x_t", [D, 2, 4 * NQ])
            w1_top = sb(setup, "w1_top", [D, H])
            w1_ab = sb(setup, "w1_ab", [D, 2 * H])
            b1_bc = sb(setup, "b1_bc", [P, H])
            r_raw = sb(setup, "r_raw", [RH + 1, 384])
            zero = sb(setup, "zero", [W, H])
            gmin = sb(setup, "gmin", [NQ, GQ])
            gmax = sb(setup, "gmax", [NQ, GQ])
            span = sb(setup, "span", [NQ, 1])
            span_row = sb(setup, "span_row", [P, NQ])
            span_i = sb(setup, "span_i", [P, 1], I32)
            rtmp = sb(setup, "rtmp", [RH + 1, 64])
            iota_i = sb(setup, "iota_i", [P, W], I32)
            iotc_i = sb(setup, "iotc_i", [P, 1], I32)
            ps = [pb(setup, f"ps_setup{i}") for i in range(4)]
            NB4 = NC // 4
            weights_in = sem("weights_in")
            x_in = sem("x_in")
            dst_in = sem("dst_in")
            src_in = sem("src_in")
            fills = sem("fills")
            base_out = sem("base_out")
            base_in = sem("base_in")
            tables_out = sem("tables_out")
            gmin_ready = sem("gmin_ready")
            span_ready = sem("span_ready")
            src_ready = sem("src_ready")
            xt_made = sem("xt_made")
            xt_copied = sem("xt_copied")
            ab_made = sem("ab_made")
            ab_copied = sem("ab_copied")
            idx_tr = sem("idx_tr")
            idx_copied = sem("idx_copied")
            n_w = 11

            with nc.Block() as block:
                @block.sync
                def _(sp):
                    sp.dma_start(rows_i[:, :], t["dst"].rearrange("(q n) -> q n", q=NQ)).then_inc(dst_in, 16)
                    sp.dma_start(x_nodes[:, :], t["x"].rearrange("(q c) d -> q (c d)", q=NQ)).then_inc(x_in, 16)
                    sp.wait_ge(fills, 8)
                    for dst, src in (
                        (w1_top[:, :], t["L0_gnn_W1"][0:D, :]),
                        (w1_ab[:, H:2 * H], t["L0_gnn_W1"][D:2 * D, :]),
                        (w2_sb[:, :], t["L0_gnn_W2"]),
                        (w3_sb[:, :], t["L0_gnn_W3"]),
                        (w4_sb[0:H, 0:D], t["L0_gnn_W4"]),
                        (w4_sb[H:H + 1, 0:D], t["L0_gnn_b4"].rearrange("(a n) -> a n", a=1)),
                        (b2_col[:, :], t["L0_gnn_b2"].rearrange("(n a) -> n a", a=1)),
                        (r_w1[0:RH, :], t["L1_gnn_w1"].rearrange("a n -> n a")),
                        (r_b1[0:RH, :], t["L1_gnn_b1"].rearrange("(n a) -> n a", a=1)),
                        (r_raw[0:RH, :], t["L1_gnn_w2"]),
                        (r_raw[RH:RH + 1, :], t["L1_gnn_b2"].rearrange("(a n) -> a n", a=1)),
                    ):
                        sp.dma_start(dst, src).then_inc(weights_in, 16)
                    sp.dma_start(rows2_i[:, :], t["src"].rearrange("(q n) -> q n", q=NQ)).then_inc(src_in, 16)
                    sp.wait_ge(gmin_ready, 1)
                    sp.wait_ge(span_ready, 1)
                    sp.dma_start(base_dram.rearrange("a (q k) -> (a q) k", q=NQ), gmin[:, :]).then_inc(base_out, 16)
                    sp.dma_start(span_dram.rearrange("a (q k) -> (a q) k", q=NQ), span[:, :]).then_inc(base_out, 16)
                    sp.wait_ge(base_out, 32)
                    sp.dma_start(base_bc[:, :], base_dram.broadcast_to([P, GROUPS])).then_inc(base_in, 16)
                    sp.dma_start(span_row[:, :], span_dram.broadcast_to([P, NQ])).then_inc(base_in, 16)
                    sp.wait_ge(ab_copied, NB4)
                    sp.dma_start(a_table[0:NODES, :].rearrange("(q c) h -> q (c h)", q=NQ), ab[:, 0, :]).then_inc(tables_out, 16)
                    sp.dma_start(b_table.rearrange("(q c) h -> q (c h)", q=NQ), ab[:, 1, :]).then_inc(tables_out, 16)
                    sp.dma_start(a_table[NODES:PADN, :], zero[:, :]).then_inc(tables_out, 16)
                    sp.wait_ge(tables_out, 48)

                @block.gpsimd
                def _(pool):
                    nc.gpsimd.memset(ident[:, :], 0.0).then_inc(setup_ids, 1)
                    nc.gpsimd.memset(sum16[:, :, :], 1.0).then_inc(sum16_step, 1)
                    nc.gpsimd.iota(iota_i[:, :], pattern=[[1, W]], base=0, channel_multiplier=0).then_inc(setup_ids, 1)
                    nc.gpsimd.iota(iotc_i[:, :], pattern=[[0, 1]], base=0, channel_multiplier=1).then_inc(setup_ids, 1)
                    pool.wait_ge(setup_ids, 3)
                    nc.gpsimd.affine_select(out=ident[:, :], in_=ident[:, :], compare_op=ALU.not_equal, fill=1.0,
                                            base=0, pattern=[[-1, P]], channel_multiplier=1).then_inc(setup_ids, 1)
                    pool.wait_ge(sum16_step, 1)
                    nc.gpsimd.affine_select(out=sum16[:, :, :], in_=sum16[:, :, :], compare_op=ALU.is_ge, fill=0.0,
                                            base=16 * (ROWS - MUL), pattern=[[P, CH], [-16, D]], channel_multiplier=1).then_inc(sum16_step, 1)
                    pool.wait_ge(sum16_step, 2)
                    nc.gpsimd.affine_select(out=sum16[:, :, :], in_=sum16[:, :, :], compare_op=ALU.is_ge, fill=0.0,
                                            base=15 - 16 * (ROWS - MUL), pattern=[[-P, CH], [16, D]], channel_multiplier=-1).then_inc(sum16_step, 1)

                @block.scalar
                def _(act):
                    act.dma_start(b1_bc[:, :], spread(t["L0_gnn_b1"], 0, P)).then_inc(loaded, 16)
                    act.dma_start(b3_bc[:, :], spread(t["L0_gnn_b3"], 0, P)).then_inc(loaded, 16)
                    act.wait_ge(src_in, 16)
                    nc.scalar.activation(rows2_f, rows2_i[:, :], ACT.Copy).then_inc(src_ready, 1)
                    for b in range(NB4):
                        act.wait_ge(xt_made, b + 1)
                        if b >= 2:
                            act.wait_ge(ab_made, b - 1)
                        nc.scalar.copy(x_t[:, b % 2, :], ps[b % 2][0:D, 0:4 * NQ]).then_inc(xt_copied, 1)

                @block.vector
                def _(dve):
                    nc.vector.memset(w4_sb[:, :], 0.0).then_inc(link_v, 1)
                    memo["v"] += 1
                    dve.wait_ge(link_v, memo["v"])
                    nc.vector.memset(w4_sb[H:H + 1, D:D + 1], 1.0).then_inc(fills, 4)
                    nc.vector.memset(r_w1[:, :], 0.0).then_inc(fills, 1)
                    nc.vector.memset(r_b1[:, :], 1.0).then_inc(fills, 1)
                    link(nc.vector.memset(r_w2[:, :], 0.0))
                    nc.vector.memset(one_col[:, :], 1.0)
                    nc.vector.memset(zero[:, :], 0.0).then_inc(fills, 1)
                    nc.vector.memset(eps_col[:, :], EPS).then_inc(fills, 1)
                    dve.wait_ge(setup_ids, 3)
                    nc.vector.tensor_copy(iota_row[:, :], iota_i[:, :])
                    link(nc.vector.tensor_copy(iota_col[:, :], iotc_i[:, :]))
                    dve.wait_ge(dst_in, 16)
                    link(nc.vector.tensor_copy(rows_f[:, :], rows_i[:, :]))
                    groups = rows_f[:, :].rearrange("q (k e) -> q k e", k=GQ)
                    nc.vector.tensor_reduce(gmin[:, :], groups, AX.X, ALU.min).then_inc(gmin_ready, 1)
                    link(nc.vector.tensor_reduce(gmax[:, :], groups, AX.X, ALU.max))
                    dve.wait_ge(gmin_ready, 1)
                    link(nc.vector.tensor_tensor(gmax[:, :], gmax[:, :], gmin[:, :], ALU.subtract))
                    nc.vector.tensor_reduce(span[:, :], gmax[:, :], AX.X, ALU.max).then_inc(span_ready, 1)
                    dve.wait_ge(weights_in, 16 * n_w)
                    nc.vector.tensor_tensor(w1_ab[:, 0:H], w1_top[:, :], w1_ab[:, H:2 * H], ALU.subtract).then_inc(dve_setup, 1)
                    mix = r_w2[0:RH + 1, 0:256].rearrange("h (x u s v) -> h x u s v", x=2, u=8, s=2)
                    vec = r_w2[0:RH + 1, 256:384].rearrange("h (u t v) -> h u t v", u=8, t=2)
                    k3 = r_raw[:, 192:384].rearrange("h (u v k) -> h u v k", u=8, v=8)

                    def flat(g):
                        return r_raw[:, 64 * g:64 * g + 64].rearrange("h (u v) -> h u v", u=8)

                    rt = rtmp[:, :].rearrange("h (u v) -> h u v", u=8)
                    link(nc.vector.tensor_scalar(rt, k3[:, :, :, 2], -A2 / 3.0, None, ALU.mult))
                    nc.vector.tensor_scalar(mix[:, 0, :, 0, :], flat(2), A10, None, ALU.mult)
                    nc.vector.tensor_scalar(mix[:, 0, :, 1, :], k3[:, :, :, 2], A2, None, ALU.mult)
                    nc.vector.tensor_scalar(mix[:, 1, :, 0, :], flat(0), A00, None, ALU.mult)
                    nc.vector.tensor_scalar(mix[:, 1, :, 1, :], flat(1), A01, None, ALU.mult)
                    nc.vector.scalar_tensor_tensor(out=vec[:, :, 0, :], in0=k3[:, :, :, 0], scalar=A110, in1=rt,
                                                   op0=ALU.mult, op1=ALU.add)
                    link(nc.vector.tensor_scalar(vec[:, :, 1, :], k3[:, :, :, 1], A111, None, ALU.mult))
                    dve.wait_ge(base_in, 32)
                    link(nc.vector.tensor_copy(base_i[:, :], base_bc[0:1, :]))
                    nc.vector.tensor_scalar(base_col[:, :], base_bc[0:W, :], iota_col[0:W, :], None, ALU.add)
                    link(nc.vector.tensor_reduce(span_row[:, 0:1], span_row[:, :], AX.X, ALU.max))
                    link(nc.vector.tensor_copy(span_i[:, :], span_row[:, 0:1]))
                    link(nc.vector.tensor_scalar(span_i[:, :], span_i[:, :], 6, None, ALU.logical_shift_right))
                    link(nc.vector.tensor_scalar(sweeps_i[:, :], span_i[:, :], 1, None, ALU.add))
                    link(nc.vector.tensor_scalar(moved[:, :], sweeps_i[:, :], float(W), None, ALU.mult))
                    dve.wait_ge(loaded, 32)
                    bias4 = spread(b1_bc[0:NQ, :], 1, 4)
                    for b in range(NB4):
                        dve.wait_ge(ab_made, b + 1)
                        pv = ps[2 + b % 2][0:NQ, :].rearrange("q (c z h) -> q c z h", c=4, z=2)
                        av = ab[:, :, b * 4 * H:(b + 1) * 4 * H].rearrange("q z (c h) -> q z c h", c=4)
                        nc.vector.tensor_tensor(av[:, 0], pv[:, :, 0, :], bias4, ALU.add)
                        nc.vector.tensor_copy(av[:, 1], pv[:, :, 1, :]).then_inc(ab_copied, 1)
                    for b in range(2 * 7):
                        n = min(4, RQ - 4 * (b % 7))
                        dve.wait_ge(idx_tr, b + 1)
                        target = (dst_rel, src_f)[b // 7][:, :].rearrange("p (q k) -> p k q", k=RQ)
                        nc.vector.tensor_copy(target[:, 4 * (b % 7):4 * (b % 7) + n, :],
                                              ps[b % 2][:, 0:n * NQ].rearrange("p (k q) -> p k q", k=n)).then_inc(idx_copied, 1)
                    dve.wait_ge(idx_copied, 14)
                    rel = dst_rel[:, :].rearrange("p (g j) -> p g j", j=GT)
                    link(nc.vector.tensor_tensor(rel, rel, spread(base_bc[:, :], 2, GT),
                                                 ALU.subtract))

                @block.tensor
                def _(pe):
                    pe.wait_ge(setup_ids, 4)
                    pe.wait_ge(x_in, 16)
                    pe.wait_ge(dve_setup, 1)

                    def columns(b):
                        pe.wait_ge(xt_copied, b + 1)
                        if b >= 2:
                            pe.wait_ge(ab_copied, b - 1)
                        for j in range(4):
                            last = nc.tensor.matmul(ps[2 + b % 2][0:NQ, j * 2 * H:(j + 1) * 2 * H],
                                                    x_t[:, b % 2, j * NQ:(j + 1) * NQ], w1_ab[:, :], start=True, stop=True)
                        last.then_inc(ab_made, 1)

                    for b in range(NB4):
                        if b >= 2:
                            pe.wait_ge(xt_copied, b - 1)
                        for j in range(4):
                            c = 4 * b + j
                            last = nc.tensor.transpose(ps[b % 2][0:D, j * NQ:(j + 1) * NQ],
                                                       x_nodes[:, c * D:(c + 1) * D], ident[0:NQ, 0:NQ])
                        last.then_inc(xt_made, 1)
                        if b >= 1:
                            columns(b - 1)
                    columns(NB4 - 1)
                    pe.wait_ge(gmin_ready, 1)
                    pe.wait_ge(src_ready, 1)
                    pe.wait_ge(xt_copied, NB4)
                    for b in range(2 * 7):
                        rows = (rows_f[:, :], rows2_f)[b // 7]
                        if b >= 2:
                            pe.wait_ge(idx_copied, b - 1)
                        for j in range(min(4, RQ - 4 * (b % 7))):
                            k = 4 * (b % 7) + j
                            last = nc.tensor.transpose(ps[b % 2][:, j * NQ:(j + 1) * NQ], rows[:, k * P:(k + 1) * P],
                                                       ident[0:NQ, 0:NQ])
                        last.then_inc(idx_tr, 1)

        acc = sb(ctx, "acc", [H + 1, PADN])

        gathers_begun = sem("gathers_begun")

        def move_windows(dve, swept):
            nc.vector.tensor_scalar(dst_rel[:, :], dst_rel[:, :], float(-W), None, ALU.add)
            nc.vector.tensor_scalar(base_col[:, :], base_col[:, :], float(W), None, ALU.add)
            nc.vector.tensor_scalar(base_i[:, :], base_i[:, :], W, NODES, ALU.add, ALU.min).then_inc(swept, 1)

        l0 = ExitStack()
        with l0:
            dst_t = sb(l0, "dst_t", [W, U, GE], I32)
            a_win = sb(l0, "a_win", [W, U, H])
            b_rows = sb(l0, "b_rows", [P, U, GT, H])
            pick_t = sb(l0, "pick_t", [W, U, GE])
            pick = sb(l0, "pick", [P, U, GT, W])
            h1 = sb(l0, "h1", [H, U, GE])
            h2 = sb(l0, "h2", [H2, U, GE])
            h3_raw = sb(l0, "h3_raw", [P, U, GT * H])
            h3 = sb(l0, "h3", [P, U, GT, H + 1])
            ps_h1 = [pb(l0, "ps_h1a"), pb(l0, "ps_h1b")]
            ps_h2 = [pb(l0, "ps_h2a"), pb(l0, "ps_h2b")]
            ps_h3 = pb(l0, "ps_h3")
            ps_sum = pb(l0, "ps_sum0")
            dst_t_in = [sem(f"dst_t_in{u}") for u in range(U)]
            a_win_in = [sem(f"a_win_in{u}") for u in range(U)]
            b_rows_in = [sem(f"b_rows_in{u}") for u in range(U)]
            idx_ready = sem("idx_ready")
            pick_t_made = sem("pick_t_made")
            pick_made = sem("pick_made")
            h1_made = sem("h1_made")
            h1_relu = sem("h1_relu")
            h2_made = sem("h2_made")
            h2_relu = sem("h2_relu")
            h3_made = sem("h3_made")
            h3_biased = sem("h3_biased")
            h3_relu = sem("h3_relu")
            sum_made = sem("sum_made")
            sum_added = sem("sum_added")
            swept = sem("swept")
            cleared = sem("cleared")
            halves = ((0, SPLIT), (SPLIT, GT))

            with nc.Block() as block:
                @block.sync
                def _(sp):
                    dst_rows = t["dst"].unsqueeze(0)
                    sweeps = sp.value_load(sweeps_i[0:1, 0:1], min_val=1, max_val=256)
                    with sp.Fori(0, sweeps) as s:
                        sp.wait_ge(swept, s + 1)
                        for b, k in turns(sp, 0):
                            g = b * U + k
                            wait_groups(sp, pick_t_made, s, g - U + 1)
                            sp.dma_start(dst_t[:, k, :], dst_rows[:, bass.ds(g * GE, GE)].broadcast_to([W, GE]))\
                                .then_inc(dst_t_in[k], 16)
                            wait_groups(sp, h1_made, s, g - U + 1)
                            base = sp.value_load(base_i[0:1, bass.ds(g, 1)], min_val=0, max_val=NODES)
                            sp.dma_start(a_win[:, k, :], a_table[bass.ds(base, W), :]).then_inc(a_win_in[k], 16)

                @block.gpsimd
                def _(pool):
                    sweeps = pool.value_load(sweeps_i[0:1, 0:1], min_val=1, max_val=256)
                    with pool.Fori(0, sweeps) as s:
                        pool.wait_ge(swept, s + 1)
                        for b, k in turns(pool, 0):
                            g = b * U + k
                            wait_groups(pool, idx_ready, s, g + 1)
                            wait_groups(pool, h1_made, s, g - U + 1)
                            pool.sem_inc(gathers_begun, 1)
                            for j in range(GT):
                                nc.gpsimd.indirect_dma_start(
                                    out=b_rows[:, k, j, :], out_offset=None, in_=b_table,
                                    in_offset=bass.IndirectOffsetOnAxis(ap=idx[:, k, j:j + 1], axis=0),
                                ).then_inc(b_rows_in[k], 16)

                @block.scalar
                def _(act):
                    sweeps = act.value_load(sweeps_i[0:1, 0:1], min_val=1, max_val=256)
                    with act.Fori(0, sweeps) as s:
                        act.wait_ge(swept, s + 1)
                        for b, k in turns(act, 4):
                            g = b * U + k
                            if live(b, k, 0):
                                wait_slot(act, b_rows_in, s, b - 1, k, 0, GT)
                                nc.scalar.activation(idx[:, k, :], src_f[:, bass.ds(g * GT, GT)], ACT.Copy).then_inc(idx_ready, 1)
                            if live(b, k, 2):
                                z = slot(k, 2)
                                wait_groups(act, h1_made, s, g - 2 + 1)
                                wait_groups(act, h2_made, s, g - 2 - U + 1)
                                for (lo, hi), ps in zip(halves, ps_h1):
                                    last = nc.scalar.activation(h1[:, z, lo * P:hi * P], ps[0:H, 0:(hi - lo) * P], ACT.Relu)
                                last.then_inc(h1_relu, 1)
                            if live(b, k, 3):
                                z = slot(k, 3)
                                wait_groups(act, h2_made, s, g - 3 + 1)
                                wait_groups(act, h3_made, s, g - 3 - U + 1)
                                for (lo, hi), ps in zip(halves, ps_h2):
                                    last = nc.scalar.activation(h2[:, z, lo * P:hi * P], ps[:, 0:(hi - lo) * P], ACT.Relu,
                                                                bias=b2_col[:, :])
                                last.then_inc(h2_relu, 1)
                            if live(b, k, 4):
                                z = slot(k, 4)
                                wait_groups(act, h3_biased, s, g - 4 + 1)
                                wait_groups(act, sum_made, s, g - 4 - U + 1)
                                nc.scalar.activation(h3[:, z, :, 0:H], h3_raw[:, z, :].rearrange("p (j h) -> p j h", j=GT),
                                                     ACT.Relu).then_inc(h3_relu, 1)

                @block.tensor
                def _(pe):
                    sweeps = pe.value_load(sweeps_i[0:1, 0:1], min_val=1, max_val=256)
                    with pe.Fori(0, sweeps) as s:
                        pe.wait_ge(swept, s + 1)
                        for b, k in turns(pe, 3):
                            g = b * U + k
                            if live(b, k, 0):
                                wait_groups(pe, pick_t_made, s, g + 1)
                                wait_slot(pe, a_win_in, s, b, k, 0)
                                wait_slot(pe, b_rows_in, s, b, k, 0, GT)
                                wait_groups(pe, h1_relu, s, g)
                                for (lo, hi), ps in zip(halves, ps_h1):
                                    for j in range(lo, hi):
                                        nc.tensor.matmul(ps[0:H, (j - lo) * P:(j - lo + 1) * P], b_rows[:, k, j, :],
                                                         ident[:, :], start=(j == lo), stop=False)
                                    last = nc.tensor.matmul(ps[0:H, 0:(hi - lo) * P], a_win[:, k, :], pick_t[:, k, lo * P:hi * P],
                                                            start=False, stop=True)
                                last.then_inc(h1_made, 1)
                            if live(b, k, 1):
                                z = slot(k, 1)
                                wait_groups(pe, h1_relu, s, g - 1 + 1)
                                wait_groups(pe, h2_relu, s, g - 1)
                                for (lo, hi), ps in zip(halves, ps_h2):
                                    last = nc.tensor.matmul(ps[:, 0:(hi - lo) * P], w2_sb[:, :], h1[:, z, lo * P:hi * P],
                                                            start=True, stop=True)
                                last.then_inc(h2_made, 1)
                            if live(b, k, 2):
                                z = slot(k, 2)
                                wait_groups(pe, h2_relu, s, g - 2 + 1)
                                wait_groups(pe, h3_biased, s, g - 2)
                                for j in range(GT):
                                    last = nc.tensor.matmul(ps_h3[:, j * H:(j + 1) * H], h2[:, z, j * P:(j + 1) * P], w3_sb[:, :],
                                                            start=True, stop=True)
                                last.then_inc(h3_made, 1)
                            if live(b, k, 3):
                                z = slot(k, 3)
                                wait_groups(pe, h3_relu, s, g - 3 + 1)
                                wait_groups(pe, pick_made, s, g - 3 + 1)
                                wait_groups(pe, sum_added, s, g - 3)
                                if isinstance(b, int) and b == 0:
                                    pe.wait_ge(cleared, 2)
                                for j in range(GT):
                                    last = nc.tensor.matmul(ps_sum[0:H + 1, 0:W], h3[:, z, j, :], pick[:, z, j, :],
                                                            start=(j == 0), stop=(j == GT - 1))
                                last.then_inc(sum_made, 1)

                @block.vector
                def _(dve):
                    nc.vector.memset(h3[:, :, :, H:H + 1], 1.0).then_inc(cleared, 1)
                    nc.vector.memset(acc[:, :], 0.0).then_inc(cleared, 1)
                    dve.wait_ge(cleared, 2)
                    dve.sem_inc(swept, 1)
                    sweeps = dve.value_load(sweeps_i[0:1, 0:1], min_val=1, max_val=256)
                    with dve.Fori(0, sweeps) as s:
                        dve.wait_ge(swept, s + 1)
                        for b, k in turns(dve, 4):
                            g = b * U + k
                            if live(b, k, 0):
                                wait_slot(dve, dst_t_in, s, b, k, 0)
                                wait_groups(dve, h1_made, s, g - U + 1)
                                nc.vector.tensor_scalar(pick_t[:, k, :], dst_t[:, k, :], base_col[:, bass.ds(g, 1)], None,
                                                        ALU.is_equal).then_inc(pick_t_made, 1)
                                wait_groups(dve, sum_made, s, g - U + 1)
                                nc.vector.tensor_tensor(pick[:, k], spread(dst_rel[:, bass.ds(g * GT, GT)], 2, W),
                                                        spread(iota_row[:, :], 1, GT), ALU.is_equal).then_inc(pick_made, 1)
                            if live(b, k, 3):
                                z = slot(k, 3)
                                wait_groups(dve, h3_made, s, g - 3 + 1)
                                wait_groups(dve, h3_relu, s, g - 3 - U + 1)
                                nc.vector.tensor_tensor(h3_raw[:, z, :].rearrange("p (j h) -> p j h", j=GT),
                                                        ps_h3[:, 0:GT * H].rearrange("p (j h) -> p j h", j=GT),
                                                        spread(b3_bc[:, :], 1, GT), ALU.add).then_inc(h3_biased, 1)
                            if live(b, k, 4):
                                base = dve.value_load(base_i[0:1, bass.ds(g - 4, 1)], min_val=0, max_val=NODES)
                                wait_groups(dve, sum_made, s, g - 4 + 1)
                                wait_groups(dve, sum_added, s, g - 4)
                                nc.vector.tensor_tensor(acc[:, bass.ds(base, W)], acc[:, bass.ds(base, W)],
                                                        ps_sum[0:H + 1, 0:W], ALU.add).then_inc(sum_added, 1)
                        wait_groups(dve, sum_added, s, GROUPS)
                        move_windows(dve, swept)

        def node_step(last):
            step = ExitStack()
            n_out = D if last else D + 1
            tag = "1" if last else "0"
            chunks = [(c, min(15, NC - c)) for c in range(0, NC, 15)]
            with step:
                y = sb(step, "y" + tag, [NQ, NC, n_out])
                sq = sb(step, "sq" + tag, [NQ, NC, D])
                stat = sb(step, "stat" + tag, [NQ, 4, NC])
                ps = [pb(step, f"ps_node{tag}{i}") for i in range(2)]
                out_made = sem("out_made" + tag)
                out_copied = sem("out_copied" + tag)
                spread_made = sem("spread_made" + tag)
                root_made = sem("root_made" + tag)
                normed = sem("normed" + tag)
                stored = sem("stored" + tag)
                with nc.Block() as block:
                    @block.tensor
                    def _(pe):
                        for n, (c0, cn) in enumerate(chunks):
                            if n >= 2:
                                pe.wait_ge(out_copied, n - 1)
                            for c in range(c0, c0 + cn):
                                lo = (c - c0) * n_out
                                if last:
                                    mm = nc.tensor.matmul(ps[n % 2][0:NQ, lo:lo + n_out], acc[0:D, c:NODES:NC],
                                                          ident[0:D, 0:D], start=True, stop=True)
                                else:
                                    mm = nc.tensor.matmul(ps[n % 2][0:NQ, lo:lo + n_out], acc[:, c:NODES:NC],
                                                          w4_sb[:, :], start=True, stop=True)
                            mm.then_inc(out_made, 1)

                    @block.scalar
                    def _(act):
                        act.wait_ge(spread_made, 1)
                        nc.scalar.activation(stat[:, 2, :], stat[:, 1, :], ACT.Sqrt, bias=eps_col[0:NQ, :], scale=1.0 / D)\
                            .then_inc(root_made, 1)

                    @block.vector
                    def _(dve):
                        for n, (c0, cn) in enumerate(chunks):
                            dve.wait_ge(out_made, n + 1)
                            nc.vector.tensor_copy(y[:, c0:c0 + cn, :], ps[n % 2][0:NQ, 0:cn * n_out].rearrange("q (c d) -> q c d", c=cn))\
                                .then_inc(out_copied, 1)
                        dve.wait_ge(out_copied, len(chunks))
                        yd = y[:, :, 0:D]
                        xv = x_nodes[:, :].rearrange("q (c d) -> q c d", c=NC)
                        if not last:
                            link(nc.vector.tensor_scalar(stat[:, 0, :], y[:, :, D], 1.0, None, ALU.max))
                            link(nc.vector.reciprocal(stat[:, 3, :], stat[:, 0, :]))
                            link(nc.vector.tensor_tensor(yd, yd, spread(stat[:, 3, :], 2, D), ALU.mult))
                        link(nc.vector.tensor_tensor(yd, yd, xv, ALU.add))
                        link(nc.vector.tensor_reduce(stat[:, 0, :], yd, AX.X, ALU.add))
                        link(nc.vector.tensor_scalar(stat[:, 0, :], stat[:, 0, :], 1.0 / D, None, ALU.mult))
                        link(nc.vector.tensor_tensor(yd, yd, spread(stat[:, 0, :], 2, D), ALU.subtract))
                        link(nc.vector.tensor_tensor(sq[:, :, :], yd, yd, ALU.mult))
                        nc.vector.tensor_reduce(stat[:, 1, :], sq[:, :, :], AX.X, ALU.add).then_inc(spread_made, 1)
                        dve.wait_ge(root_made, 1)
                        link(nc.vector.reciprocal(stat[:, 3, :], stat[:, 2, :]))
                        nc.vector.tensor_tensor(xv, yd, spread(stat[:, 3, :], 2, D), ALU.mult).then_inc(normed, 1)

                    @block.sync
                    def _(sp):
                        target = out if last else x1_table
                        sp.wait_ge(normed, 1)
                        sp.dma_start(target.rearrange("(q c) d -> q (c d)", q=NQ), x_nodes[:, :]).then_inc(stored, 16)
                        sp.wait_ge(stored, 16)

        node_step(False)

        unit = sb(ctx, "unit", [P, 3, TILES])
        prep = ExitStack()
        with prep:
            attr_rows = sb(prep, "attr_rows", [NQ, RQ, P, 3])
            norm = sb(prep, "norm", [P, TILES])
            part = sb(prep, "part", [P, TILES])
            ps = [pb(prep, f"ps_unit{i}") for i in range(2)]
            attr_in = sem("attr_in")
            axis_turned = sem("axis_turned")
            axis_copied = sem("axis_copied")
            squares_made = sem("squares_made")
            norm_made = sem("norm_made")
            cleared1 = sem("cleared1")
            axes = (1, 2, 0)
            turns_n = [(n, c, 4 * m, min(4, RQ - 4 * m)) for n, c in enumerate(axes) for m in range(7)]
            with nc.Block() as block:
                @block.sync
                def _(sp):
                    sp.dma_start(attr_rows[:, :, :, :].rearrange("q k p c -> q (k p c)"),
                                 t["edge_attr_3"].rearrange("(q n) c -> q (n c)", q=NQ)).then_inc(attr_in, 16)

                @block.tensor
                def _(pe):
                    pe.wait_ge(attr_in, 16)
                    for m, (n, c, k0, kn) in enumerate(turns_n):
                        if m >= 2:
                            pe.wait_ge(axis_copied, m - 1)
                        for k in range(k0, k0 + kn):
                            last = nc.tensor.transpose(ps[m % 2][:, (k - k0) * NQ:(k - k0 + 1) * NQ], attr_rows[:, k, :, c],
                                                       ident[0:NQ, 0:NQ])
                        last.then_inc(axis_turned, 1)

                @block.scalar
                def _(act):
                    act.wait_ge(squares_made, 1)
                    nc.scalar.activation(norm[:, :], norm[:, :], ACT.Sqrt).then_inc(norm_made, 1)

                @block.vector
                def _(dve):
                    nc.vector.memset(acc[0:D, :], 0.0)
                    nc.vector.tensor_scalar(dst_rel[:, :], dst_rel[:, :], moved[:, 0:1], None, ALU.add)
                    nc.vector.tensor_copy(base_i[:, :], base_bc[0:1, :])
                    for m, (n, c, k0, kn) in enumerate(turns_n):
                        dve.wait_ge(axis_turned, m + 1)
                        nc.vector.tensor_copy(unit[:, n, :].rearrange("p (q k) -> p k q", k=RQ)[:, k0:k0 + kn, :],
                                              ps[m % 2][:, 0:kn * NQ].rearrange("p (k q) -> p k q", k=kn)).then_inc(axis_copied, 1)
                    dve.wait_ge(axis_copied, len(turns_n))
                    nc.vector.tensor_tensor(norm[:, :], unit[:, 0, :], unit[:, 0, :], ALU.mult)
                    link(nc.vector.tensor_tensor(part[:, :], unit[:, 1, :], unit[:, 1, :], ALU.mult))
                    link(nc.vector.tensor_tensor(norm[:, :], norm[:, :], part[:, :], ALU.add))
                    link(nc.vector.tensor_tensor(part[:, :], unit[:, 2, :], unit[:, 2, :], ALU.mult))
                    nc.vector.tensor_tensor(norm[:, :], norm[:, :], part[:, :], ALU.add).then_inc(squares_made, 1)
                    dve.wait_ge(norm_made, 1)
                    link(nc.vector.reciprocal(norm[:, :], norm[:, :]))
                    link(nc.vector.tensor_tensor(unit[:, :, :], unit[:, :, :], spread(norm[:, :], 1, 3), ALU.mult))

        l1 = ExitStack()
        with l1:
            hid = sb(l1, "hid", [P, U, GE])
            f_rows = sb(l1, "f_rows", [P, U, GT, D])
            pick = sb(l1, "pick1", [P, U, GT, W])
            gap2 = sb(l1, "gap2", [P, GT, W])
            n5 = sb(l1, "n5", [P, U, GT, 5])
            f5 = sb(l1, "f5", [P, U, GT, 5, MUL])
            mix_in = sb(l1, "mix_in", [P, U, GT, 2, MUL])
            vec_in = sb(l1, "vec_in", [P, U, GT, 3, 2, MUL])
            dots = sb(l1, "dots", [P, GT, MUL, 3])
            cross = sb(l1, "cross", [P, 2, GT, 3, MUL])
            prods = sb(l1, "prods", [P, GT, 40 * 16])
            sums = sb(l1, "sums", [P, U, GT, ROWS])
            side = sb(l1, "side", [P, U, GT, D])
            node_prods = sb(l1, "node_prods", [P, U, CH, W])
            r_banks = [pb(l1, f"ps_r{j}") for j in range(4)]
            ps_r = [r_banks[j] for j in (0, 1, 2, 3, 1)]
            r_before = [(-1, 0), (-1, 4), (-1, 2), (-1, 3), (0, 1)]
            ps_np = [pb(l1, f"ps_np{i}") for i in range(3)]
            ps_sum = pb(l1, "ps_sum1")
            np_place = [ps_np[i][:, 0:CH * W] for i in (0, 1, 0, 1, 2)]
            weight_in = [sem(f"weight_in{u}") for u in range(U)]
            f_rows_in = [sem(f"f_rows_in{u}") for u in range(U)]
            idx_ready = sem("idx_ready1")
            hid_made = sem("hid_made")
            n5_made = sem("n5_made")
            f_copied = sem("f_copied")
            r_made = sem("r_made")
            r_used = sem("r_used")
            gap2_made = sem("gap2_made")
            picked = sem("picked")
            dots_made = sem("dots_made")
            cross_made = sem("cross_made")
            mix_made = sem("mix_made")
            vec_made = sem("vec_made")
            summed = sem("summed")
            along_made = sem("along_made")
            out0_copied = sem("out0_copied")
            side_made = sem("side_made")
            np_made = sem("np_made")
            np_copied = sem("np_copied")
            sum_made = sem("sum_made1")
            sum_added = sem("sum_added1")
            swept = sem("swept1")

            def wait_tile(eng, sem, sweep, g, j):
                if not isinstance(g, int) or g >= 0:
                    eng.wait_ge(sem, (sweep * GROUPS + g) * GT + (j + 1))

            def wait_sums(eng, sweep, g, half):
                if not isinstance(g, int) or g >= 0:
                    eng.wait_ge(summed, (sweep * GROUPS + g) * 2 + (half + 1))

            with nc.Block() as block:
                @block.sync
                def _(sp):
                    weights = t["edge_weight"].unsqueeze(0)
                    sweeps = sp.value_load(sweeps_i[0:1, 0:1], min_val=1, max_val=256)
                    with sp.Fori(0, sweeps) as s:
                        sp.wait_ge(swept, s + 1)
                        for b, k in turns(sp, 0):
                            g = b * U + k
                            wait_tile(sp, r_made, s, g - U, GT - 1)
                            sp.dma_start(hid[0:RH + 1, k, :], weights[:, bass.ds(g * GE, GE)].broadcast_to([RH + 1, GE]))\
                                .then_inc(weight_in[k], 16)

                @block.gpsimd
                def _(pool):
                    sweeps = pool.value_load(sweeps_i[0:1, 0:1], min_val=1, max_val=256)
                    with pool.Fori(0, sweeps) as s:
                        pool.wait_ge(swept, s + 1)
                        for b, k in turns(pool, 4):
                            g = b * U + k
                            if live(b, k, 3):
                                z = slot(k, 3)
                                wait_groups(pool, n5_made, s, g - 3 + 1)
                                wait_groups(pool, f_copied, s, g - 3 + 1)
                                wait_tile(pool, r_used, s, g - 3 - U, GT - 1)
                                wait_groups(pool, vec_made, s, g - 3)
                                nc.gpsimd.tensor_tensor(cross[:, 0], f5[:, z, :, 2:5, :], spread(n5[:, z, :, 1:4], 3, MUL), ALU.mult)
                                nc.gpsimd.tensor_tensor(cross[:, 1], f5[:, z, :, 1:4, :], spread(n5[:, z, :, 2:5], 3, MUL), ALU.mult)\
                                    .then_inc(cross_made, 1)
                                wait_groups(pool, cross_made, s, g - 3 + 1)
                                nc.gpsimd.tensor_tensor(vec_in[:, z, :, :, 1, :], cross[:, 0], cross[:, 1], ALU.subtract).then_inc(vec_made, 1)
                            if live(b, k, 0):
                                wait_groups(pool, idx_ready, s, g + 1)
                                wait_groups(pool, f_copied, s, g - U + 1)
                                pool.sem_inc(gathers_begun, 1)
                            for j in range(GT if live(b, k, 0) else 0):
                                nc.gpsimd.indirect_dma_start(
                                    out=f_rows[:, k, j, :], out_offset=None, in_=x1_table,
                                    in_offset=bass.IndirectOffsetOnAxis(ap=idx[:, k, j:j + 1], axis=0),
                                ).then_inc(f_rows_in[k], 16)
                            if live(b, k, 4):
                                z = slot(k, 4)
                                wait_groups(pool, summed, s, g - 4 + 1, 2)
                                wait_groups(pool, sum_made, s, g - 4 - U + 1)
                                nc.gpsimd.tensor_tensor(side[:, z, :, MUL:D].rearrange("p j (u o) -> p j u o", o=3),
                                                        spread(sums[:, z, :, 0:MUL], 3, 3), spread(n5[:, z, :, 0:3], 2, MUL),
                                                        ALU.mult).then_inc(along_made, 1)

                @block.scalar
                def _(act):
                    sweeps = act.value_load(sweeps_i[0:1, 0:1], min_val=1, max_val=256)
                    with act.Fori(0, sweeps) as s:
                        act.wait_ge(swept, s + 1)
                        for b, k in turns(act, 5):
                            g = b * U + k
                            if live(b, k, 0):
                                wait_slot(act, f_rows_in, s, b - 1, k, 0, GT)
                                nc.scalar.activation(idx[:, k, :], src_f[:, bass.ds(g * GT, GT)], ACT.Copy).then_inc(idx_ready, 1)
                            if live(b, k, 1):
                                z = slot(k, 1)
                                wait_groups(act, along_made, s, g - 1 - U + 1)
                                nv = unit[:, :, bass.ds(g * GT - GT, GT)].rearrange("p o j -> p j o")
                                nc.scalar.copy(n5[:, z, :, 0:3], nv)
                                nc.scalar.copy(n5[:, z, :, 3:5], nv[:, :, 0:2]).then_inc(n5_made, 1)
                            if live(b, k, 2):
                                z = slot(k, 2)
                                wait_slot(act, f_rows_in, s, b, k, 2, GT)
                                wait_tile(act, r_used, s, g - 2 - U, GT - 1)
                                f1 = f_rows[:, z, :, MUL:D].rearrange("p j (v o) -> p j o v", v=MUL)
                                nc.scalar.copy(mix_in[:, z, :, 0, :], f_rows[:, z, :, 0:MUL])
                                nc.scalar.copy(f5[:, z, :, 0:3, :], f1)
                                nc.scalar.copy(f5[:, z, :, 3:5, :], f1[:, :, 0:2, :])
                                nc.scalar.copy(vec_in[:, z, :, :, 0, :], f1).then_inc(f_copied, 1)
                                wait_slot(act, weight_in, s, b, k, 2)
                                nc.scalar.activation(hid[0:RH + 1, z, :], hid[0:RH + 1, z, :], ACT.Relu, bias=r_b1[:, :], scale=r_w1[:, :])\
                                    .then_inc(hid_made, 1)
                            if live(b, k, 3):
                                z = slot(k, 3)
                                wait_groups(act, picked, s, g - 3)
                                for j in range(GT):
                                    mm = nc.scalar.activation(gap2[:, j, :], iota_row[:, :], ACT.Square, scale=-1.0,
                                                              bias=dst_rel[:, bass.ds(g * GT + (j - 3 * GT), 1)])
                                mm.then_inc(gap2_made, 1)
                                wait_groups(act, sum_made, s, g - 3 - U + 1)
                                wait_groups(act, gap2_made, s, g - 3 + 1)
                                nc.scalar.activation(pick[:, z], gap2[:, :, :], ACT.Relu, scale=-1.0, bias=one_col[:, :])\
                                    .then_inc(picked, 1)
                            if live(b, k, 5):
                                z = slot(k, 5)
                                wait_tile(act, np_made, s, g - 5, GT - 1)
                                wait_groups(act, sum_made, s, g - 5 - U + 1)
                                nc.scalar.copy(node_prods[:, z].rearrange("p c w -> p (c w)"), np_place[z]).then_inc(np_copied, 1)
                                wait_groups(act, summed, s, g - 5 + 1, 2)
                                nc.scalar.copy(side[:, z, :, 0:MUL], sums[:, z, :, MUL:2 * MUL]).then_inc(out0_copied, 1)

                @block.tensor
                def _(pe):
                    sweeps = pe.value_load(sweeps_i[0:1, 0:1], min_val=1, max_val=256)

                    def sum_products(s, b, k, lag, j):
                        z = slot(k, lag)
                        g = b * U + k - lag
                        wait_tile(pe, r_used, s, g, j)
                        if j == 0:
                            wait_groups(pe, picked, s, g + 1)
                            wait_groups(pe, np_copied, s, g - 1)
                        for c in range(CH):
                            mm = nc.tensor.matmul(np_place[z][:, c * W:(c + 1) * W], prods[:, j, 16 * ROWS + c * P:16 * ROWS + (c + 1) * P],
                                                  pick[:, z, j, :], start=(j == 0 and c == 0),
                                                  stop=(j == GT - 1 and c == CH - 1))
                        mm.then_inc(np_made, 1)

                    with pe.Fori(0, sweeps) as s:
                        pe.wait_ge(swept, s + 1)
                        for b, k in turns(pe, 3):
                            g = b * U + k
                            if live(b, k, 0):
                                wait_groups(pe, hid_made, s, g + 1)
                            for j in range(GT):
                                if live(b, k, 0):
                                    back, before = r_before[j]
                                    wait_tile(pe, r_used, s, g + back, before)
                                    nc.tensor.matmul(ps_r[j][:, 0:384], hid[:, k, j * P:(j + 1) * P], r_w2[:, :],
                                                     start=True, stop=True).then_inc(r_made, 1)
                                behind = 1 if j < TILE_LAG else 0
                                if live(b, k, behind):
                                    sum_products(s, b, k, behind, (j - TILE_LAG) % GT)
                                if j == 1 and live(b, k, 3):
                                    z = slot(k, 3)
                                    wait_groups(pe, np_copied, s, g - 3 + 1)
                                    wait_groups(pe, side_made, s, g - 3 + 1)
                                    wait_groups(pe, out0_copied, s, g - 3 + 1)
                                    wait_groups(pe, sum_added, s, g - 3)
                                    for c in range(CH):
                                        nc.tensor.matmul(ps_sum[0:D, 0:W], sum16[:, c, :], node_prods[:, z, c, :],
                                                         start=(c == 0), stop=False)
                                    for i in range(GT):
                                        last = nc.tensor.matmul(ps_sum[0:D, 0:W], side[:, z, i, :], pick[:, z, i, :],
                                                                start=False, stop=(i == GT - 1))
                                    last.then_inc(sum_made, 1)

                @block.vector
                def _(dve):
                    nc.vector.memset(hid[RH:P, :, :], 0.0).then_inc(swept, 1)
                    sweeps = dve.value_load(sweeps_i[0:1, 0:1], min_val=1, max_val=256)
                    with dve.Fori(0, sweeps) as s:
                        dve.wait_ge(swept, s + 1)
                        for b, k in turns(dve, 4):
                            g = b * U + k

                            def products(j):
                                if not live(b, k, 1):
                                    return
                                z = slot(k, 1)
                                if j == 0:
                                    wait_groups(dve, mix_made, s, g - 1 + 1)
                                    wait_groups(dve, vec_made, s, g - 1 + 1)
                                    wait_groups(dve, sum_made, s, g - 1 - U + 1)
                                wait_sums(dve, s, g - 2, 0 if j < 3 else 1)
                                wait_tile(dve, r_made, s, g - 1, j)
                                wait_tile(dve, np_made, s, g - 2, j)
                                nc.vector.tensor_tensor(
                                    prods[:, j, 0:256].rearrange("p (r s) -> p r s", s=16),
                                    ps_r[j][:, 0:256].rearrange("p (r s) -> p r s", s=16),
                                    spread(mix_in[:, z, j].rearrange("p s v -> p (s v)"), 1, 16), ALU.mult)
                                nc.vector.tensor_tensor(
                                    prods[:, j, 256:640].rearrange("p (u o s) -> p u o s", u=MUL, o=3),
                                    spread(ps_r[j][:, 256:384].rearrange("p (u s) -> p u s", u=MUL), 2, 3),
                                    spread(vec_in[:, z, j].rearrange("p o t v -> p o (t v)"), 1, MUL), ALU.mult)\
                                    .then_inc(r_used, 1)

                            def sum_rows(lag, half):
                                if not live(b, k, lag):
                                    return
                                z = slot(k, lag)
                                lo, hi = ((0, 3), (3, GT))[half]
                                wait_tile(dve, r_used, s, g - lag, hi - 1)
                                nc.vector.tensor_reduce(sums[:, z, lo:hi, :],
                                                        prods[:, lo:hi, 0:16 * ROWS].rearrange("p j (r s) -> p j r s", s=16),
                                                        AX.X, ALU.add).then_inc(summed, 1)

                            products(0)
                            sum_rows(2, 1)
                            if live(b, k, 3):
                                z = slot(k, 3)
                                wait_groups(dve, along_made, s, g - 3 + 1)
                                more = side[:, z, :, MUL:ROWS - MUL]
                                nc.vector.tensor_tensor(more, more, sums[:, z, :, 2 * MUL:ROWS], ALU.add).then_inc(side_made, 1)
                            products(1)
                            if live(b, k, 0):
                                wait_groups(dve, n5_made, s, g + 1)
                                wait_groups(dve, f_copied, s, g + 1)
                                nc.vector.tensor_tensor(dots[:, :, :, :], f5[:, k, :, 0:3, :].rearrange("p j o v -> p j v o"),
                                                        spread(n5[:, k, :, 0:3], 2, MUL), ALU.mult).then_inc(dots_made, 1)
                            products(2)
                            if live(b, k, 4):
                                base = dve.value_load(base_i[0:1, bass.ds(g - 4, 1)], min_val=0, max_val=NODES)
                                wait_groups(dve, sum_made, s, g - 4 + 1)
                                wait_groups(dve, sum_added, s, g - 4)
                                nc.vector.tensor_tensor(acc[0:D, bass.ds(base, W)], acc[0:D, bass.ds(base, W)],
                                                        ps_sum[0:D, 0:W], ALU.add).then_inc(sum_added, 1)
                            products(3)
                            sum_rows(1, 0)
                            if live(b, k, 0):
                                wait_groups(dve, dots_made, s, g + 1)
                                nc.vector.tensor_reduce(mix_in[:, k, :, 1, :], dots[:, :, :, :], AX.X, ALU.add).then_inc(mix_made, 1)
                            products(4)
                        wait_groups(dve, sum_added, s, GROUPS)
                        move_windows(dve, swept)

        node_step(True)


_INS = ["x", "src", "dst", "edge_attr_3", "edge_weight", "L0_gnn_W1", "L0_gnn_b1", "L0_gnn_W2", "L0_gnn_b2",
        "L0_gnn_W3", "L0_gnn_b3", "L0_gnn_W4", "L0_gnn_b4", "L1_gnn_w1", "L1_gnn_b1", "L1_gnn_w2", "L1_gnn_b2"]


def kernel(**inputs):
    import numpy as _np
    import concourse.bacc as _bacc
    from concourse import mybir as _mybir
    from concourse.bass_utils import run_bass_kernel_spmd as _run

    nc = _bacc.Bacc("TRN2", target_bir_lowering=False, num_devices=1)
    arrays, tensors = {}, {}
    for name in _INS:
        a = _np.ascontiguousarray(inputs[name])
        arrays[f"in_{name}_dram"] = a
        tensors[name] = nc.dram_tensor(f"in_{name}_dram", a.shape, _mybir.dt.from_np(a.dtype), kind="ExternalInput").ap()
    out = nc.dram_tensor("out_dram", (NODES, D), FP32, kind="ExternalOutput").ap()
    build(nc, tensors, out)
    r = _run(nc, [arrays], core_ids=[0])
    return r.results[0]["out_dram"]
```

```python
import concourse.bass as bass
from concourse import mybir
from contextlib import ExitStack
from math import pi, sqrt

FP32 = mybir.dt.float32
I32 = mybir.dt.int32
U32 = mybir.dt.uint32
ALU = mybir.AluOpType
ACT = mybir.ActivationFunctionType
AX = mybir.AxisListType

NODES, EDGES = 12500, 400000
D, H, H2 = 32, 64, 128
MUL, RH = 8, 64
P = 128
TILES = EDGES // P
GT = 5
GE = GT * P
GROUPS = TILES // GT
W = 64
U = 5
BLOCKS = GROUPS // U
NQ, NC = 125, 100
RQ = TILES // NQ
GQ = GROUPS // NQ
PADN = NODES + W
SPLIT = 3
ROWS = 24
CH = (40 - ROWS) * 16 // P
SPLIT_SUMS = 4
TILE_LAG = 3
EPS = 1e-5
assert TILES * P == EDGES and GROUPS * GT == TILES and BLOCKS * U == GROUPS and NQ * NC == NODES

N0 = sqrt(4 * pi) / sqrt(MUL * 2)
N1 = sqrt(4 * pi) * sqrt(3.0) / sqrt(MUL + MUL * 3)
Y0 = 0.5 / sqrt(pi)
C1 = sqrt(3.0 / (4.0 * pi))
C2A = 0.5 * sqrt(15.0 / pi)
A00 = N0 * Y0
A01 = N0 * C1 / sqrt(3.0)
A10 = N1 * C1 / sqrt(3.0)
A110 = N1 * Y0 / sqrt(3.0)
A111 = N1 * C1 / sqrt(6.0)
A2 = N1 * C2A / sqrt(10.0)


def spread(ap, axis, n):
    ap = ap.unsqueeze(axis)
    shape = list(ap.shape)
    shape[axis] = n
    return ap.broadcast_to(shape)


def turns(eng, lag):
    peeled = 2 if lag else 1
    for b in range(peeled):
        for k in range(U):
            yield b, k
    with eng.Fori(peeled, BLOCKS) as b:
        for k in range(U):
            yield b, k
    for k in range(lag):
        yield BLOCKS, k


def live(b, k, lag):
    return not isinstance(b, int) or 0 <= b * U + k - lag < GROUPS


def slot(k, lag):
    return (k - lag) % U


def wait_groups(eng, sem, sweep, count, per_group=1):
    if not isinstance(count, int) or count > 0:
        eng.wait_ge(sem, (sweep * GROUPS + count) * per_group)


def wait_slot(eng, sem, sweep, b, k, lag, dmas=1):
    rounds = b + (k - lag) // U + 1
    if not isinstance(rounds, int) or rounds > 0:
        eng.wait_ge(sem[slot(k, lag)], (sweep * BLOCKS + rounds) * (16 * dmas))


def build(nc, t, out):
    ctx = ExitStack()
    with ctx:
        def sb(c, name, shape, dt=FP32):
            return c.enter_context(nc.sbuf_tensor(name, shape, dt))

        def pb(c, name):
            return c.enter_context(nc.psum_tensor(name, [128, 512], FP32))

        def sem(name):
            return ctx.enter_context(nc.semaphore(name))

        a_table = nc.dram_tensor("a_table", [PADN, H], FP32, kind="Internal").ap()
        b_table = nc.dram_tensor("b_table", [NODES, H], FP32, kind="Internal").ap()
        x1_table = nc.dram_tensor("x1_table", [NODES, D], FP32, kind="Internal").ap()
        base_dram = nc.dram_tensor("base_dram", [1, GROUPS], FP32, kind="Internal").ap()
        span_dram = nc.dram_tensor("span_dram", [1, NQ], FP32, kind="Internal").ap()

        ident = sb(ctx, "ident", [P, P])
        iota_row = sb(ctx, "iota_row", [P, W])
        iota_col = sb(ctx, "iota_col", [P, 1])
        eps_col = sb(ctx, "eps_col", [P, 1])
        one_col = sb(ctx, "one_col", [P, 1])
        dst_rel = sb(ctx, "dst_rel", [P, TILES])
        src_f = sb(ctx, "src_f", [P, TILES])
        x_nodes = sb(ctx, "x_nodes", [NQ, NC * D])
        base_bc = sb(ctx, "base_bc", [P, GROUPS])
        base_col = sb(ctx, "base_col", [W, GROUPS])
        base_i = sb(ctx, "base_i", [1, GROUPS], I32)
        sweeps_i = sb(ctx, "sweeps_i", [P, 1], I32)
        moved = sb(ctx, "moved", [P, 1])
        w2_sb = sb(ctx, "w2_sb", [H, H2])
        w3_sb = sb(ctx, "w3_sb", [H2, H])
        w4_sb = sb(ctx, "w4_sb", [H + 1, D + 1])
        b2_col = sb(ctx, "b2_col", [H2, 1])
        b3_bc = sb(ctx, "b3_bc", [P, H])
        r_w1 = sb(ctx, "r_w1", [RH + 1, 1])
        r_b1 = sb(ctx, "r_b1", [RH + 1, 1])
        r_w2 = sb(ctx, "r_w2", [P, 384])
        sum16 = sb(ctx, "sum16", [P, CH, D])
        idx = sb(ctx, "idx", [P, U, GT], U32)

        setup_ids = sem("setup_ids")
        sum16_step = sem("sum16_step")
        bias_in = sem("bias_in")
        link_v = sem("link_v")
        w1_made = sem("w1_made")
        memo = {"v": 0}

        def link(ins):
            memo["v"] += 1
            ins.then_inc(link_v, 1)
            nc.vector.wait_ge(link_v, memo["v"])

        setup = ExitStack()
        with setup:
            rows_i = sb(setup, "rows_i", [NQ, RQ * P], I32)
            rows_f = sb(setup, "rows_f", [NQ, RQ * P])
            rows2_i = sb(setup, "rows2_i", [NQ, RQ * P], I32)
            rows2_f = rows2_i[:, :].bitcast(FP32)
            ab = sb(setup, "ab", [NQ, 2, NC * H])
            x_t = sb(setup, "x_t", [4 * D, 2, NQ])
            w1_top = sb(setup, "w1_top", [4 * D, H])
            w1_ab = sb(setup, "w1_ab", [4 * D, 4, 2 * H])
            b1_bc = sb(setup, "b1_bc", [P, H])
            r_raw = sb(setup, "r_raw", [RH + 1, 384])
            zero = sb(setup, "zero", [W, H])
            gmin = sb(setup, "gmin", [NQ, GQ])
            gmax = sb(setup, "gmax", [NQ, GQ])
            span = sb(setup, "span", [NQ, 1])
            span_row = sb(setup, "span_row", [P, NQ])
            span_i = sb(setup, "span_i", [P, 1], I32)
            rtmp = sb(setup, "rtmp", [RH + 1, 64])
            iota_i = sb(setup, "iota_i", [P, W], I32)
            iotc_i = sb(setup, "iotc_i", [P, 1], I32)
            ps = [pb(setup, f"ps_setup{i}") for i in range(4)]
            NB4 = NC // 4
            w1_in = sem("w1_in")
            w1_clear = sem("w1_clear")
            weights_in = sem("weights_in")
            x_in = sem("x_in")
            dst_in = sem("dst_in")
            src_in = sem("src_in")
            fills = sem("fills")
            base_out = sem("base_out")
            base_in = sem("base_in")
            tables_out = sem("tables_out")
            gmin_ready = sem("gmin_ready")
            span_ready = sem("span_ready")
            src_ready = sem("src_ready")
            xt_made = sem("xt_made")
            xt_copied = sem("xt_copied")
            ab_made = sem("ab_made")
            ab_copied = sem("ab_copied")
            idx_tr = sem("idx_tr")
            idx_copied = sem("idx_copied")
            n_w = 9

            with nc.Block() as block:
                @block.sync
                def _(sp):
                    sp.dma_start(rows_i[:, :], t["dst"].rearrange("(q n) -> q n", q=NQ)).then_inc(dst_in, 16)
                    sp.dma_start(x_nodes[:, :], t["x"].rearrange("(q c) d -> q (c d)", q=NQ)).then_inc(x_in, 16)
                    sp.wait_ge(w1_clear, 1)
                    for j in range(4):
                        rows = slice(j * D, (j + 1) * D)
                        sp.dma_start(w1_top[rows, :], t["L0_gnn_W1"][0:D, :]).then_inc(w1_in, 16)
                        sp.dma_start(w1_ab[rows, j, H:2 * H], t["L0_gnn_W1"][D:2 * D, :]).then_inc(w1_in, 16)
                    sp.wait_ge(fills, 8)
                    for dst, src in (
                        (w2_sb[:, :], t["L0_gnn_W2"]),
                        (w3_sb[:, :], t["L0_gnn_W3"]),
                        (w4_sb[0:H, 0:D], t["L0_gnn_W4"]),
                        (w4_sb[H:H + 1, 0:D], t["L0_gnn_b4"].rearrange("(a n) -> a n", a=1)),
                        (b2_col[:, :], t["L0_gnn_b2"].rearrange("(n a) -> n a", a=1)),
                        (r_w1[0:RH, :], t["L1_gnn_w1"].rearrange("a n -> n a")),
                        (r_b1[0:RH, :], t["L1_gnn_b1"].rearrange("(n a) -> n a", a=1)),
                        (r_raw[0:RH, :], t["L1_gnn_w2"]),
                        (r_raw[RH:RH + 1, :], t["L1_gnn_b2"].rearrange("(a n) -> a n", a=1)),
                    ):
                        sp.dma_start(dst, src).then_inc(weights_in, 16)
                    sp.dma_start(rows2_i[:, :], t["src"].rearrange("(q n) -> q n", q=NQ)).then_inc(src_in, 16)
                    sp.wait_ge(gmin_ready, 1)
                    sp.wait_ge(span_ready, 1)
                    sp.dma_start(base_dram.rearrange("a (q k) -> (a q) k", q=NQ), gmin[:, :]).then_inc(base_out, 16)
                    sp.dma_start(span_dram.rearrange("a (q k) -> (a q) k", q=NQ), span[:, :]).then_inc(base_out, 16)
                    sp.wait_ge(base_out, 32)
                    sp.dma_start(base_bc[:, :], base_dram.broadcast_to([P, GROUPS])).then_inc(base_in, 16)
                    sp.dma_start(span_row[:, :], span_dram.broadcast_to([P, NQ])).then_inc(base_in, 16)
                    sp.dma_start(a_table[NODES:PADN, :], zero[:, :]).then_inc(tables_out, 16)
                    rows_of = "(q c) h -> q c h"
                    piece = NB4 // 5
                    for b in range(0, NB4, piece):
                        sp.wait_ge(ab_copied, b + piece)
                        cols = slice(4 * b, 4 * (b + piece))
                        for table, z in ((b_table, 1), (a_table[0:NODES, :], 0)):
                            sp.dma_start(table.rearrange(rows_of, q=NQ)[:, cols, :],
                                         ab[:, z, :].rearrange("q (c h) -> q c h", c=NC)[:, cols, :]).then_inc(tables_out, 16)
                    sp.wait_ge(tables_out, 16 * (1 + 2 * 5))

                @block.gpsimd
                def _(pool):
                    nc.gpsimd.memset(ident[:, :], 0.0).then_inc(setup_ids, 1)
                    nc.gpsimd.memset(sum16[:, :, :], 1.0).then_inc(sum16_step, 1)
                    nc.gpsimd.iota(iota_i[:, :], pattern=[[1, W]], base=0, channel_multiplier=0).then_inc(setup_ids, 1)
                    nc.gpsimd.iota(iotc_i[:, :], pattern=[[0, 1]], base=0, channel_multiplier=1).then_inc(setup_ids, 1)
                    pool.wait_ge(setup_ids, 3)
                    nc.gpsimd.affine_select(out=ident[:, :], in_=ident[:, :], compare_op=ALU.not_equal, fill=1.0,
                                            base=0, pattern=[[-1, P]], channel_multiplier=1).then_inc(setup_ids, 1)
                    pool.wait_ge(sum16_step, 1)
                    nc.gpsimd.affine_select(out=sum16[:, :, :], in_=sum16[:, :, :], compare_op=ALU.is_ge, fill=0.0,
                                            base=16 * (ROWS - MUL), pattern=[[P, CH], [-16, D]], channel_multiplier=1).then_inc(sum16_step, 1)
                    pool.wait_ge(sum16_step, 2)
                    nc.gpsimd.affine_select(out=sum16[:, :, :], in_=sum16[:, :, :], compare_op=ALU.is_ge, fill=0.0,
                                            base=15 - 16 * (ROWS - MUL), pattern=[[-P, CH], [16, D]], channel_multiplier=-1).then_inc(sum16_step, 1)

                @block.scalar
                def _(act):
                    act.dma_start(b1_bc[:, :], spread(t["L0_gnn_b1"], 0, P)).then_inc(bias_in, 16)
                    act.dma_start(b3_bc[:, :], spread(t["L0_gnn_b3"], 0, P)).then_inc(bias_in, 16)
                    act.wait_ge(src_in, 16)
                    nc.scalar.activation(rows2_f, rows2_i[:, :], ACT.Copy).then_inc(src_ready, 1)
                    for b in range(NB4):
                        act.wait_ge(xt_made, b + 1)
                        if b >= 2:
                            act.wait_ge(ab_made, b - 1)
                        nc.scalar.copy(x_t[:, b % 2, :], ps[b % 2][:, 0:NQ]).then_inc(xt_copied, 1)

                @block.vector
                def _(dve):
                    nc.vector.memset(w1_ab[:, :, :], 0.0).then_inc(w1_clear, 1)
                    nc.vector.memset(w4_sb[:, :], 0.0).then_inc(link_v, 1)
                    memo["v"] += 1
                    dve.wait_ge(link_v, memo["v"])
                    nc.vector.memset(w4_sb[H:H + 1, D:D + 1], 1.0).then_inc(fills, 4)
                    nc.vector.memset(r_w1[:, :], 0.0).then_inc(fills, 1)
                    nc.vector.memset(r_b1[:, :], 1.0).then_inc(fills, 1)
                    link(nc.vector.memset(r_w2[:, :], 0.0))
                    nc.vector.memset(one_col[:, :], 1.0)
                    nc.vector.memset(zero[:, :], 0.0).then_inc(fills, 1)
                    nc.vector.memset(eps_col[:, :], EPS).then_inc(fills, 1)
                    dve.wait_ge(setup_ids, 3)
                    nc.vector.tensor_copy(iota_row[:, :], iota_i[:, :])
                    link(nc.vector.tensor_copy(iota_col[:, :], iotc_i[:, :]))
                    dve.wait_ge(dst_in, 16)
                    link(nc.vector.tensor_copy(rows_f[:, :], rows_i[:, :]))
                    groups = rows_f[:, :].rearrange("q (k e) -> q k e", k=GQ)
                    nc.vector.tensor_reduce(gmin[:, :], groups, AX.X, ALU.min).then_inc(gmin_ready, 1)
                    link(nc.vector.tensor_reduce(gmax[:, :], groups, AX.X, ALU.max))
                    dve.wait_ge(gmin_ready, 1)
                    link(nc.vector.tensor_tensor(gmax[:, :], gmax[:, :], gmin[:, :], ALU.subtract))
                    nc.vector.tensor_reduce(span[:, :], gmax[:, :], AX.X, ALU.max).then_inc(span_ready, 1)
                    dve.wait_ge(w1_in, 16 * 8)
                    for j in range(4):
                        rows = slice(j * D, (j + 1) * D)
                        nc.vector.tensor_tensor(w1_ab[rows, j, 0:H], w1_top[rows, :], w1_ab[rows, j, H:2 * H], ALU.subtract)\
                            .then_inc(w1_made, 1)
                    dve.wait_ge(weights_in, 16 * n_w)
                    mix = r_w2[0:RH + 1, 0:256].rearrange("h (x u s v) -> h x u s v", x=2, u=8, s=2)
                    vec = r_w2[0:RH + 1, 256:384].rearrange("h (u t v) -> h u t v", u=8, t=2)
                    k3 = r_raw[:, 192:384].rearrange("h (u v k) -> h u v k", u=8, v=8)

                    def flat(g):
                        return r_raw[:, 64 * g:64 * g + 64].rearrange("h (u v) -> h u v", u=8)

                    rt = rtmp[:, :].rearrange("h (u v) -> h u v", u=8)
                    link(nc.vector.tensor_scalar(rt, k3[:, :, :, 2], -A2 / 3.0, None, ALU.mult))
                    nc.vector.tensor_scalar(mix[:, 0, :, 0, :], flat(2), A10, None, ALU.mult)
                    nc.vector.tensor_scalar(mix[:, 0, :, 1, :], k3[:, :, :, 2], A2, None, ALU.mult)
                    nc.vector.tensor_scalar(mix[:, 1, :, 0, :], flat(0), A00, None, ALU.mult)
                    nc.vector.tensor_scalar(mix[:, 1, :, 1, :], flat(1), A01, None, ALU.mult)
                    nc.vector.scalar_tensor_tensor(out=vec[:, :, 0, :], in0=k3[:, :, :, 0], scalar=A110, in1=rt,
                                                   op0=ALU.mult, op1=ALU.add)
                    link(nc.vector.tensor_scalar(vec[:, :, 1, :], k3[:, :, :, 1], A111, None, ALU.mult))
                    dve.wait_ge(base_in, 32)
                    link(nc.vector.tensor_copy(base_i[:, :], base_bc[0:1, :]))
                    nc.vector.tensor_scalar(base_col[:, :], base_bc[0:W, :], iota_col[0:W, :], None, ALU.add)
                    link(nc.vector.tensor_reduce(span_row[:, 0:1], span_row[:, :], AX.X, ALU.max))
                    link(nc.vector.tensor_copy(span_i[:, :], span_row[:, 0:1]))
                    link(nc.vector.tensor_scalar(span_i[:, :], span_i[:, :], 6, None, ALU.logical_shift_right))
                    link(nc.vector.tensor_scalar(sweeps_i[:, :], span_i[:, :], 1, None, ALU.add))
                    link(nc.vector.tensor_scalar(moved[:, :], sweeps_i[:, :], float(W), None, ALU.mult))
                    dve.wait_ge(bias_in, 32)
                    bias4 = spread(b1_bc[0:NQ, :], 1, 4)
                    for b in range(NB4):
                        dve.wait_ge(ab_made, b + 1)
                        pv = ps[2 + b % 2][0:NQ, :].rearrange("q (c z h) -> q c z h", c=4, z=2)
                        av = ab[:, :, b * 4 * H:(b + 1) * 4 * H].rearrange("q z (c h) -> q z c h", c=4)
                        nc.vector.tensor_tensor(av[:, 0], pv[:, :, 0, :], bias4, ALU.add)
                        nc.vector.tensor_copy(av[:, 1], pv[:, :, 1, :]).then_inc(ab_copied, 1)
                    for b in range(2 * 7):
                        n = min(4, RQ - 4 * (b % 7))
                        dve.wait_ge(idx_tr, b + 1)
                        target = (dst_rel, src_f)[b // 7][:, :].rearrange("p (q k) -> p k q", k=RQ)
                        nc.vector.tensor_copy(target[:, 4 * (b % 7):4 * (b % 7) + n, :],
                                              ps[b % 2][:, 0:n * NQ].rearrange("p (k q) -> p k q", k=n)).then_inc(idx_copied, 1)
                    dve.wait_ge(idx_copied, 14)
                    rel = dst_rel[:, :].rearrange("p (g j) -> p g j", j=GT)
                    link(nc.vector.tensor_tensor(rel, rel, spread(base_bc[:, :], 2, GT),
                                                 ALU.subtract))

                @block.tensor
                def _(pe):
                    pe.wait_ge(setup_ids, 4)
                    pe.wait_ge(x_in, 16)
                    pe.wait_ge(w1_made, 4)

                    def columns(b):
                        pe.wait_ge(xt_copied, b + 1)
                        if b >= 2:
                            pe.wait_ge(ab_copied, b - 1)
                        nc.tensor.matmul(ps[2 + b % 2][0:NQ, :], x_t[:, b % 2, :], w1_ab[:, :, :].rearrange("d j h -> d (j h)"),
                                         start=True, stop=True).then_inc(ab_made, 1)

                    for b in range(NB4):
                        if b >= 2:
                            pe.wait_ge(xt_copied, b - 1)
                        nc.tensor.transpose(ps[b % 2][:, 0:NQ], x_nodes[:, 4 * b * D:4 * (b + 1) * D], ident[0:NQ, 0:NQ])\
                            .then_inc(xt_made, 1)
                        if b >= 1:
                            columns(b - 1)
                    columns(NB4 - 1)
                    pe.wait_ge(gmin_ready, 1)
                    pe.wait_ge(src_ready, 1)
                    pe.wait_ge(xt_copied, NB4)
                    for b in range(2 * 7):
                        rows = (rows_f[:, :], rows2_f)[b // 7]
                        if b >= 2:
                            pe.wait_ge(idx_copied, b - 1)
                        for j in range(min(4, RQ - 4 * (b % 7))):
                            k = 4 * (b % 7) + j
                            last = nc.tensor.transpose(ps[b % 2][:, j * NQ:(j + 1) * NQ], rows[:, k * P:(k + 1) * P],
                                                       ident[0:NQ, 0:NQ])
                        last.then_inc(idx_tr, 1)

        acc = sb(ctx, "acc", [H + 1, PADN])

        gathers_begun = sem("gathers_begun")

        def move_windows(dve, swept):
            nc.vector.tensor_scalar(dst_rel[:, :], dst_rel[:, :], float(-W), None, ALU.add)
            nc.vector.tensor_scalar(base_col[:, :], base_col[:, :], float(W), None, ALU.add)
            nc.vector.tensor_scalar(base_i[:, :], base_i[:, :], W, NODES, ALU.add, ALU.min).then_inc(swept, 1)

        l0 = ExitStack()
        with l0:
            dst_t = sb(l0, "dst_t", [W, U, GE], I32)
            a_win = sb(l0, "a_win", [W, U, H])
            b_rows = sb(l0, "b_rows", [P, U, GT, H])
            pick_t = sb(l0, "pick_t", [W, U, GE])
            pick = sb(l0, "pick", [P, U, GT, W])
            h1 = sb(l0, "h1", [H, U, GE])
            h2 = sb(l0, "h2", [H2, U, GE])
            h3_raw = sb(l0, "h3_raw", [P, U, GT * H])
            h3 = sb(l0, "h3", [P, U, GT, H + 1])
            ps_h1 = [pb(l0, "ps_h1a"), pb(l0, "ps_h1b")]
            ps_h2 = [pb(l0, "ps_h2a"), pb(l0, "ps_h2b")]
            ps_h3 = pb(l0, "ps_h3")
            ps_sum = pb(l0, "ps_sum0")
            dst_t_in = [sem(f"dst_t_in{u}") for u in range(U)]
            a_win_in = [sem(f"a_win_in{u}") for u in range(U)]
            b_rows_in = [sem(f"b_rows_in{u}") for u in range(U)]
            idx_ready = sem("idx_ready")
            pick_t_made = sem("pick_t_made")
            pick_made = sem("pick_made")
            h1_made = sem("h1_made")
            h1_relu = sem("h1_relu")
            h2_made = sem("h2_made")
            h2_relu = sem("h2_relu")
            h3_made = sem("h3_made")
            h3_biased = sem("h3_biased")
            h3_relu = sem("h3_relu")
            sum_made = sem("sum_made")
            sum_added = sem("sum_added")
            swept = sem("swept")
            cleared = sem("cleared")
            halves = ((0, SPLIT), (SPLIT, GT))

            with nc.Block() as block:
                @block.sync
                def _(sp):
                    dst_rows = t["dst"].unsqueeze(0)
                    sweeps = sp.value_load(sweeps_i[0:1, 0:1], min_val=1, max_val=256)
                    with sp.Fori(0, sweeps) as s:
                        sp.wait_ge(swept, s + 1)
                        for b, k in turns(sp, 0):
                            g = b * U + k
                            wait_groups(sp, pick_t_made, s, g - U + 1)
                            sp.dma_start(dst_t[:, k, :], dst_rows[:, bass.ds(g * GE, GE)].broadcast_to([W, GE]))\
                                .then_inc(dst_t_in[k], 16)
                            wait_groups(sp, h1_made, s, g - U + 1)
                            base = sp.value_load(base_i[0:1, bass.ds(g, 1)], min_val=0, max_val=NODES)
                            sp.dma_start(a_win[:, k, :], a_table[bass.ds(base, W), :]).then_inc(a_win_in[k], 16)

                @block.gpsimd
                def _(pool):
                    sweeps = pool.value_load(sweeps_i[0:1, 0:1], min_val=1, max_val=256)
                    with pool.Fori(0, sweeps) as s:
                        pool.wait_ge(swept, s + 1)
                        for b, k in turns(pool, 0):
                            g = b * U + k
                            wait_groups(pool, idx_ready, s, g + 1)
                            wait_groups(pool, h1_made, s, g - U + 1)
                            pool.sem_inc(gathers_begun, 1)
                            for j in range(GT):
                                nc.gpsimd.indirect_dma_start(
                                    out=b_rows[:, k, j, :], out_offset=None, in_=b_table,
                                    in_offset=bass.IndirectOffsetOnAxis(ap=idx[:, k, j:j + 1], axis=0),
                                ).then_inc(b_rows_in[k], 16)

                @block.scalar
                def _(act):
                    sweeps = act.value_load(sweeps_i[0:1, 0:1], min_val=1, max_val=256)
                    with act.Fori(0, sweeps) as s:
                        act.wait_ge(swept, s + 1)
                        for b, k in turns(act, 4):
                            g = b * U + k
                            if live(b, k, 0):
                                wait_slot(act, b_rows_in, s, b - 1, k, 0, GT)
                                nc.scalar.activation(idx[:, k, :], src_f[:, bass.ds(g * GT, GT)], ACT.Copy).then_inc(idx_ready, 1)
                            if live(b, k, 2):
                                z = slot(k, 2)
                                wait_groups(act, h1_made, s, g - 2 + 1)
                                wait_groups(act, h2_made, s, g - 2 - U + 1)
                                for (lo, hi), ps in zip(halves, ps_h1):
                                    last = nc.scalar.activation(h1[:, z, lo * P:hi * P], ps[0:H, 0:(hi - lo) * P], ACT.Relu)
                                last.then_inc(h1_relu, 1)
                            if live(b, k, 3):
                                z = slot(k, 3)
                                wait_groups(act, h2_made, s, g - 3 + 1)
                                wait_groups(act, h3_made, s, g - 3 - U + 1)
                                for (lo, hi), ps in zip(halves, ps_h2):
                                    last = nc.scalar.activation(h2[:, z, lo * P:hi * P], ps[:, 0:(hi - lo) * P], ACT.Relu,
                                                                bias=b2_col[:, :])
                                last.then_inc(h2_relu, 1)
                            if live(b, k, 4):
                                z = slot(k, 4)
                                wait_groups(act, h3_biased, s, g - 4 + 1)
                                wait_groups(act, sum_made, s, g - 4 - U + 1)
                                nc.scalar.activation(h3[:, z, :, 0:H], h3_raw[:, z, :].rearrange("p (j h) -> p j h", j=GT),
                                                     ACT.Relu).then_inc(h3_relu, 1)

                @block.tensor
                def _(pe):
                    sweeps = pe.value_load(sweeps_i[0:1, 0:1], min_val=1, max_val=256)
                    with pe.Fori(0, sweeps) as s:
                        pe.wait_ge(swept, s + 1)
                        for b, k in turns(pe, 3):
                            g = b * U + k
                            if live(b, k, 0):
                                wait_groups(pe, pick_t_made, s, g + 1)
                                wait_slot(pe, a_win_in, s, b, k, 0)
                                wait_slot(pe, b_rows_in, s, b, k, 0, GT)
                                wait_groups(pe, h1_relu, s, g)
                                for (lo, hi), ps in zip(halves, ps_h1):
                                    for j in range(lo, hi):
                                        nc.tensor.matmul(ps[0:H, (j - lo) * P:(j - lo + 1) * P], b_rows[:, k, j, :],
                                                         ident[:, :], start=(j == lo), stop=False)
                                    last = nc.tensor.matmul(ps[0:H, 0:(hi - lo) * P], a_win[:, k, :], pick_t[:, k, lo * P:hi * P],
                                                            start=False, stop=True)
                                last.then_inc(h1_made, 1)
                            if live(b, k, 1):
                                z = slot(k, 1)
                                wait_groups(pe, h1_relu, s, g - 1 + 1)
                                wait_groups(pe, h2_relu, s, g - 1)
                                for (lo, hi), ps in zip(halves, ps_h2):
                                    last = nc.tensor.matmul(ps[:, 0:(hi - lo) * P], w2_sb[:, :], h1[:, z, lo * P:hi * P],
                                                            start=True, stop=True)
                                last.then_inc(h2_made, 1)
                            if live(b, k, 2):
                                z = slot(k, 2)
                                wait_groups(pe, h2_relu, s, g - 2 + 1)
                                wait_groups(pe, h3_biased, s, g - 2)
                                for j in range(GT):
                                    last = nc.tensor.matmul(ps_h3[:, j * H:(j + 1) * H], h2[:, z, j * P:(j + 1) * P], w3_sb[:, :],
                                                            start=True, stop=True)
                                last.then_inc(h3_made, 1)
                            if live(b, k, 3):
                                z = slot(k, 3)
                                wait_groups(pe, h3_relu, s, g - 3 + 1)
                                wait_groups(pe, pick_made, s, g - 3 + 1)
                                wait_groups(pe, sum_added, s, g - 3)
                                if isinstance(b, int) and b == 0:
                                    pe.wait_ge(cleared, 2)
                                for j in range(GT):
                                    last = nc.tensor.matmul(ps_sum[0:H + 1, 0:W], h3[:, z, j, :], pick[:, z, j, :],
                                                            start=(j == 0), stop=(j == GT - 1))
                                last.then_inc(sum_made, 1)

                @block.vector
                def _(dve):
                    nc.vector.memset(h3[:, :, :, H:H + 1], 1.0).then_inc(cleared, 1)
                    dve.sem_inc(swept, 1)
                    nc.vector.memset(acc[:, :], 0.0).then_inc(cleared, 1)
                    dve.wait_ge(cleared, 2)
                    sweeps = dve.value_load(sweeps_i[0:1, 0:1], min_val=1, max_val=256)
                    with dve.Fori(0, sweeps) as s:
                        dve.wait_ge(swept, s + 1)
                        for b, k in turns(dve, 4):
                            g = b * U + k
                            if live(b, k, 0):
                                wait_slot(dve, dst_t_in, s, b, k, 0)
                                wait_groups(dve, h1_made, s, g - U + 1)
                                nc.vector.tensor_scalar(pick_t[:, k, :], dst_t[:, k, :], base_col[:, bass.ds(g, 1)], None,
                                                        ALU.is_equal).then_inc(pick_t_made, 1)
                                wait_groups(dve, sum_made, s, g - U + 1)
                                nc.vector.tensor_tensor(pick[:, k], spread(dst_rel[:, bass.ds(g * GT, GT)], 2, W),
                                                        spread(iota_row[:, :], 1, GT), ALU.is_equal).then_inc(pick_made, 1)
                            if live(b, k, 3):
                                z = slot(k, 3)
                                wait_groups(dve, h3_made, s, g - 3 + 1)
                                wait_groups(dve, h3_relu, s, g - 3 - U + 1)
                                nc.vector.tensor_tensor(h3_raw[:, z, :].rearrange("p (j h) -> p j h", j=GT),
                                                        ps_h3[:, 0:GT * H].rearrange("p (j h) -> p j h", j=GT),
                                                        spread(b3_bc[:, :], 1, GT), ALU.add).then_inc(h3_biased, 1)
                            if live(b, k, 4):
                                base = dve.value_load(base_i[0:1, bass.ds(g - 4, 1)], min_val=0, max_val=NODES)
                                wait_groups(dve, sum_made, s, g - 4 + 1)
                                wait_groups(dve, sum_added, s, g - 4)
                                nc.vector.tensor_tensor(acc[:, bass.ds(base, W)], acc[:, bass.ds(base, W)],
                                                        ps_sum[0:H + 1, 0:W], ALU.add).then_inc(sum_added, 1)
                        wait_groups(dve, sum_added, s, GROUPS)
                        move_windows(dve, swept)

        def node_step(last, beside=None):
            step = ExitStack()
            n_out = D if last else D + 1
            tag = "1" if last else "0"
            chunks = [(c, min(15, NC - c)) for c in range(0, NC, 15)]
            beside = beside or {}
            with step:
                work = sb(step, "work" + tag, [NQ, 15, D])
                stat = sb(step, "stat" + tag, [NQ, 4, NC])
                ps = [pb(step, f"ps_node{tag}{i}") for i in range(2)]
                out_made = sem("out_made" + tag)
                out_read = sem("out_read" + tag)
                spread_made = sem("spread_made" + tag)
                root_made = sem("root_made" + tag)
                normed = sem("normed" + tag)
                stored = sem("stored" + tag)
                with nc.Block() as block:
                    @block.tensor
                    def _(pe):
                        for n, (c0, cn) in enumerate(chunks):
                            if n >= 2:
                                pe.wait_ge(out_read, n - 1)
                            for c in range(c0, c0 + cn):
                                lo = (c - c0) * n_out
                                if last:
                                    mm = nc.tensor.matmul(ps[n % 2][0:NQ, lo:lo + n_out], acc[0:D, c:NODES:NC],
                                                          ident[0:D, 0:D], start=True, stop=True)
                                else:
                                    mm = nc.tensor.matmul(ps[n % 2][0:NQ, lo:lo + n_out], acc[:, c:NODES:NC],
                                                          w4_sb[:, :], start=True, stop=True)
                            mm.then_inc(out_made, 1)
                            if n == 2 and "tensor" in beside:
                                beside["tensor"](pe)

                    @block.gpsimd
                    def _(pool):
                        if "gpsimd" in beside:
                            pool.wait_ge(out_made, len(chunks))
                            beside["gpsimd"](pool)

                    @block.scalar
                    def _(act):
                        if "scalar" in beside:
                            beside["scalar"](act)
                        act.wait_ge(spread_made, len(chunks))
                        nc.scalar.activation(stat[:, 2, :], stat[:, 1, :], ACT.Sqrt, bias=eps_col[0:NQ, :], scale=1.0 / D)\
                            .then_inc(root_made, 1)

                    @block.vector
                    def _(dve):
                        xv = x_nodes[:, :].rearrange("q (c d) -> q c d", c=NC)
                        for n, (c0, cn) in enumerate(chunks):
                            span = slice(c0, c0 + cn)
                            xc = xv[:, span, :]
                            part = work[:, 0:cn, :]
                            made = ps[n % 2][0:NQ, 0:cn * n_out].rearrange("q (c d) -> q c d", c=cn)
                            dve.wait_ge(out_made, n + 1)
                            if last:
                                nc.vector.tensor_tensor(xc, made, xc, ALU.add).then_inc(out_read, 1)
                                dve.wait_ge(out_read, n + 1)
                            else:
                                link(nc.vector.tensor_scalar(stat[:, 0, span], made[:, :, D], 1.0, None, ALU.max))
                                link(nc.vector.reciprocal(stat[:, 3, span], stat[:, 0, span]))
                                nc.vector.tensor_tensor(part, made[:, :, 0:D], spread(stat[:, 3, span], 2, D), ALU.mult).then_inc(out_read, 1)
                                dve.wait_ge(out_read, n + 1)
                                link(nc.vector.tensor_tensor(xc, part, xc, ALU.add))
                            link(nc.vector.tensor_reduce(stat[:, 0, span], xc, AX.X, ALU.add))
                            link(nc.vector.tensor_scalar(stat[:, 0, span], stat[:, 0, span], 1.0 / D, None, ALU.mult))
                            link(nc.vector.tensor_tensor(xc, xc, spread(stat[:, 0, span], 2, D), ALU.subtract))
                            link(nc.vector.tensor_tensor(part, xc, xc, ALU.mult))
                            nc.vector.tensor_reduce(stat[:, 1, span], part, AX.X, ALU.add).then_inc(spread_made, 1)
                            if "vector" in beside:
                                beside["vector"](dve, n)
                        dve.wait_ge(root_made, 1)
                        link(nc.vector.reciprocal(stat[:, 3, :], stat[:, 2, :]))
                        nc.vector.tensor_tensor(xv, xv, spread(stat[:, 3, :], 2, D), ALU.mult).then_inc(normed, 1)

                    @block.sync
                    def _(sp):
                        if "sync" in beside:
                            beside["sync"](sp)
                        target = out if last else x1_table
                        sp.wait_ge(normed, 1)
                        sp.dma_start(target.rearrange("(q c) d -> q (c d)", q=NQ), x_nodes[:, :]).then_inc(stored, 16)
                        sp.wait_ge(stored, 16)

        unit = sb(ctx, "unit", [P, 3, TILES])
        prep = ExitStack()
        with prep:
            attr_room = sb(prep, "attr_room", [P, RQ * P * 3])
            attr_rows = attr_room[0:NQ, :].rearrange("q (k p c) -> q k p c", k=RQ, c=3)
            squares = attr_room[:, 0:3 * TILES].rearrange("p (o n) -> p o n", o=3)
            ps_unit = [pb(prep, f"ps_unit{i}") for i in range(4)]
            attr_in = sem("attr_in")
            axis_turned = sem("axis_turned")
            axis_copied = sem("axis_copied")
            squares_made = sem("squares_made")
            square_made = sem("square_made")
            length_made = sem("length_made")
            inverse_made = sem("inverse_made")
            axes = (1, 2, 0)
            batches = [(n, c, k, min(4, RQ - k)) for n, c in enumerate(axes) for k in range(0, RQ, 4)]
            length = squares[:, 0, :]

            def load_attr(sp):
                sp.dma_start(attr_room[0:NQ, :],
                             t["edge_attr_3"].rearrange("(q n) c -> q (n c)", q=NQ)).then_inc(attr_in, 16)

            def turn_axes(pe):
                pe.wait_ge(attr_in, 16)
                for m, (n, c, k0, kn) in enumerate(batches):
                    if m >= 4:
                        pe.wait_ge(axis_copied, m - 3)
                    for k in range(k0, k0 + kn):
                        last = nc.tensor.transpose(ps_unit[m % 4][:, (k - k0) * NQ:(k - k0 + 1) * NQ], attr_rows[:, k, :, c],
                                                   ident[0:NQ, 0:NQ])
                    last.then_inc(axis_turned, 1)

            def square_axes(act):
                for m, (n, c, k0, kn) in enumerate(batches):
                    act.wait_ge(axis_turned, m + 1)
                    nc.scalar.copy(unit[:, n, :].rearrange("p (q k) -> p k q", k=RQ)[:, k0:k0 + kn, :],
                                   ps_unit[m % 4][:, 0:kn * NQ].rearrange("p (k q) -> p k q", k=kn)).then_inc(axis_copied, 1)
                act.wait_ge(axis_copied, len(batches))
                nc.scalar.activation(squares, unit[:, :, :], ACT.Square).then_inc(squares_made, 1)
                nc.scalar.activation(dst_rel[:, :], dst_rel[:, :], ACT.Identity, bias=moved[:, 0:1])
                act.wait_ge(square_made, 1)
                nc.scalar.activation(length, length, ACT.Sqrt).then_inc(length_made, 1)

            def invert_lengths(dve, n):
                half = TILES // 2
                if n == 3:
                    dve.wait_ge(squares_made, 1)
                    link(nc.vector.tensor_tensor(length, length, squares[:, 1, :], ALU.add))
                    nc.vector.tensor_tensor(length, length, squares[:, 2, :], ALU.add).then_inc(square_made, 1)
                if n == 4:
                    dve.wait_ge(length_made, 1)
                    nc.vector.reciprocal(length[:, 0:half], length[:, 0:half])
                if n == 5:
                    nc.vector.reciprocal(length[:, half:TILES], length[:, half:TILES]).then_inc(inverse_made, 1)
                    nc.vector.tensor_copy(base_i[:, :], base_bc[0:1, :])
                if n == 6:
                    dve.wait_ge(inverse_made, 1)
                    nc.vector.tensor_tensor(unit[:, 0, :], unit[:, 0, :], length, ALU.mult)

            def clear_and_scale(pool):
                nc.gpsimd.memset(acc[0:D, :], 0.0)
                pool.wait_ge(inverse_made, 1)
                nc.gpsimd.tensor_tensor(unit[:, 1, :], unit[:, 1, :], length, ALU.mult)
                nc.gpsimd.tensor_tensor(unit[:, 2, :], unit[:, 2, :], length, ALU.mult)

            node_step(False, {"sync": load_attr, "tensor": turn_axes, "scalar": square_axes,
                              "vector": invert_lengths, "gpsimd": clear_and_scale})

        l1 = ExitStack()
        with l1:
            hid = sb(l1, "hid", [P, U, GE])
            f_rows = sb(l1, "f_rows", [P, U, GT, D])
            pick = sb(l1, "pick1", [P, U, GT, W])
            gap2 = sb(l1, "gap2", [P, GT, W])
            n5 = sb(l1, "n5", [P, U, GT, 5])
            f5 = sb(l1, "f5", [P, U, GT, 5, MUL])
            mix_in = sb(l1, "mix_in", [P, U, GT, 2, MUL])
            vec_in = sb(l1, "vec_in", [P, U, GT, 3, 2, MUL])
            dots = sb(l1, "dots", [P, GT, MUL, 3])
            cross = sb(l1, "cross", [P, 2, GT, 3, MUL])
            prods = sb(l1, "prods", [P, GT, 40 * 16])
            sums = sb(l1, "sums", [P, U, GT, ROWS])
            side = sb(l1, "side", [P, U, GT, D])
            node_prods = sb(l1, "node_prods", [P, U, CH, W])
            ps_r = l1.enter_context(nc.psum_tensor("ps_r", [P, 4, 512], FP32))
            r_bank = (0, 1, 2, 3, 2)
            r_before = [(-1, 0), (-1, 1), (-1, 4), (-1, 3), (0, 2)]
            ps_np = [pb(l1, f"ps_np{i}") for i in range(3)]
            ps_sum = pb(l1, "ps_sum1")
            np_place = [ps_np[i][:, 0:CH * W] for i in (0, 1, 0, 1, 2)]
            weight_in = [sem(f"weight_in{u}") for u in range(U)]
            f_rows_in = [sem(f"f_rows_in{u}") for u in range(U)]
            idx_ready = sem("idx_ready1")
            hid_made = sem("hid_made")
            n5_made = sem("n5_made")
            f_copied = sem("f_copied")
            r_made = sem("r_made")
            r_used = sem("r_used")
            gap2_made = sem("gap2_made")
            picked = sem("picked")
            dots_made = sem("dots_made")
            cross_made = sem("cross_made")
            mix_made = sem("mix_made")
            vec_made = sem("vec_made")
            summed = sem("summed")
            along_made = sem("along_made")
            out0_copied = sem("out0_copied")
            side_made = sem("side_made")
            np_made = sem("np_made")
            np_copied = sem("np_copied")
            sum_made = sem("sum_made1")
            sum_added = sem("sum_added1")
            swept = sem("swept1")

            def wait_tile(eng, sem, sweep, g, j):
                if not isinstance(g, int) or g >= 0:
                    eng.wait_ge(sem, (sweep * GROUPS + g) * GT + (j + 1))

            def wait_sums(eng, sweep, g, half):
                if not isinstance(g, int) or g >= 0:
                    eng.wait_ge(summed, (sweep * GROUPS + g) * 2 + (half + 1))

            with nc.Block() as block:
                @block.sync
                def _(sp):
                    weights = t["edge_weight"].unsqueeze(0)
                    sweeps = sp.value_load(sweeps_i[0:1, 0:1], min_val=1, max_val=256)
                    with sp.Fori(0, sweeps) as s:
                        sp.wait_ge(swept, s + 1)
                        for b, k in turns(sp, 0):
                            g = b * U + k
                            wait_tile(sp, r_made, s, g - U, GT - 1)
                            sp.dma_start(hid[0:RH + 1, k, :], weights[:, bass.ds(g * GE, GE)].broadcast_to([RH + 1, GE]))\
                                .then_inc(weight_in[k], 16)

                @block.gpsimd
                def _(pool):
                    sweeps = pool.value_load(sweeps_i[0:1, 0:1], min_val=1, max_val=256)
                    with pool.Fori(0, sweeps) as s:
                        pool.wait_ge(swept, s + 1)
                        for b, k in turns(pool, 5):
                            g = b * U + k
                            if live(b, k, 3):
                                z = slot(k, 3)
                                wait_groups(pool, n5_made, s, g - 3 + 1)
                                wait_groups(pool, f_copied, s, g - 3 + 1)
                                wait_tile(pool, r_used, s, g - 3 - U, GT - 1)
                                wait_groups(pool, vec_made, s, g - 3)
                                nc.gpsimd.tensor_tensor(cross[:, 0], f5[:, z, :, 2:5, :], spread(n5[:, z, :, 1:4], 3, MUL), ALU.mult)
                                nc.gpsimd.tensor_tensor(cross[:, 1], f5[:, z, :, 1:4, :], spread(n5[:, z, :, 2:5], 3, MUL), ALU.mult)\
                                    .then_inc(cross_made, 1)
                            if live(b, k, 5):
                                z = slot(k, 5)
                                wait_groups(pool, summed, s, g - 5 + 1, 2)
                                wait_groups(pool, sum_made, s, g - 5 - U + 1)
                                nc.gpsimd.tensor_tensor(side[:, z, :, MUL:D].rearrange("p j (u o) -> p j u o", o=3),
                                                        spread(sums[:, z, :, 0:MUL], 3, 3), spread(n5[:, z, :, 0:3], 2, MUL),
                                                        ALU.mult).then_inc(along_made, 1)
                            if live(b, k, 3):
                                z = slot(k, 3)
                                wait_groups(pool, cross_made, s, g - 3 + 1)
                                nc.gpsimd.tensor_tensor(vec_in[:, z, :, :, 1, :], cross[:, 0], cross[:, 1], ALU.subtract).then_inc(vec_made, 1)
                            if live(b, k, 0):
                                wait_groups(pool, idx_ready, s, g + 1)
                                wait_groups(pool, f_copied, s, g - U + 1)
                                pool.sem_inc(gathers_begun, 1)
                            for j in range(GT if live(b, k, 0) else 0):
                                nc.gpsimd.indirect_dma_start(
                                    out=f_rows[:, k, j, :], out_offset=None, in_=x1_table,
                                    in_offset=bass.IndirectOffsetOnAxis(ap=idx[:, k, j:j + 1], axis=0),
                                ).then_inc(f_rows_in[k], 16)

                @block.scalar
                def _(act):
                    sweeps = act.value_load(sweeps_i[0:1, 0:1], min_val=1, max_val=256)
                    with act.Fori(0, sweeps) as s:
                        act.wait_ge(swept, s + 1)
                        for b, k in turns(act, 5):
                            g = b * U + k
                            if live(b, k, 0):
                                wait_slot(act, f_rows_in, s, b - 1, k, 0, GT)
                                nc.scalar.activation(idx[:, k, :], src_f[:, bass.ds(g * GT, GT)], ACT.Copy).then_inc(idx_ready, 1)
                            if live(b, k, 1):
                                z = slot(k, 1)
                                wait_groups(act, along_made, s, g - 1 - U + 1)
                                nv = unit[:, :, bass.ds(g * GT - GT, GT)].rearrange("p o j -> p j o")
                                nc.scalar.copy(n5[:, z, :, 0:3], nv)
                                nc.scalar.copy(n5[:, z, :, 3:5], nv[:, :, 0:2]).then_inc(n5_made, 1)
                            if live(b, k, 2):
                                z = slot(k, 2)
                                wait_slot(act, f_rows_in, s, b, k, 2, GT)
                                wait_tile(act, r_used, s, g - 2 - U, GT - 1)
                                f1 = f_rows[:, z, :, MUL:D].rearrange("p j (v o) -> p j o v", v=MUL)
                                nc.scalar.copy(mix_in[:, z, :, 0, :], f_rows[:, z, :, 0:MUL])
                                nc.scalar.copy(f5[:, z, :, 0:3, :], f1)
                                nc.scalar.copy(f5[:, z, :, 3:5, :], f1[:, :, 0:2, :])
                                nc.scalar.copy(vec_in[:, z, :, :, 0, :], f1).then_inc(f_copied, 1)
                                wait_slot(act, weight_in, s, b, k, 2)
                                nc.scalar.activation(hid[0:RH + 1, z, :], hid[0:RH + 1, z, :], ACT.Relu, bias=r_b1[:, :], scale=r_w1[:, :])\
                                    .then_inc(hid_made, 1)
                            if live(b, k, 3):
                                z = slot(k, 3)
                                wait_groups(act, picked, s, g - 3)
                                for j in range(GT):
                                    mm = nc.scalar.activation(gap2[:, j, :], iota_row[:, :], ACT.Square, scale=-1.0,
                                                              bias=dst_rel[:, bass.ds(g * GT + (j - 3 * GT), 1)])
                                mm.then_inc(gap2_made, 1)
                                wait_groups(act, sum_made, s, g - 3 - U + 1)
                                wait_groups(act, gap2_made, s, g - 3 + 1)
                                nc.scalar.activation(pick[:, z], gap2[:, :, :], ACT.Relu, scale=-1.0, bias=one_col[:, :])\
                                    .then_inc(picked, 1)
                            if live(b, k, 5):
                                z = slot(k, 5)
                                wait_tile(act, np_made, s, g - 5, GT - 1)
                                wait_groups(act, sum_made, s, g - 5 - U + 1)
                                nc.scalar.copy(node_prods[:, z].rearrange("p c w -> p (c w)"), np_place[z]).then_inc(np_copied, 1)
                                wait_groups(act, summed, s, g - 5 + 1, 2)
                                nc.scalar.copy(side[:, z, :, 0:MUL], sums[:, z, :, MUL:2 * MUL]).then_inc(out0_copied, 1)

                @block.tensor
                def _(pe):
                    sweeps = pe.value_load(sweeps_i[0:1, 0:1], min_val=1, max_val=256)

                    def sum_products(s, b, k, lag, j):
                        z = slot(k, lag)
                        g = b * U + k - lag
                        wait_tile(pe, r_used, s, g, j)
                        if j == 0:
                            wait_groups(pe, picked, s, g + 1)
                            wait_groups(pe, np_copied, s, g - 1)
                        for c in range(CH):
                            mm = nc.tensor.matmul(np_place[z][:, c * W:(c + 1) * W], prods[:, j, 16 * ROWS + c * P:16 * ROWS + (c + 1) * P],
                                                  pick[:, z, j, :], start=(j == 0 and c == 0),
                                                  stop=(j == GT - 1 and c == CH - 1))
                        mm.then_inc(np_made, 1)

                    with pe.Fori(0, sweeps) as s:
                        pe.wait_ge(swept, s + 1)
                        for b, k in turns(pe, 3):
                            g = b * U + k
                            if live(b, k, 0):
                                wait_groups(pe, hid_made, s, g + 1)
                            for j in range(GT):
                                if live(b, k, 0):
                                    back, before = r_before[j]
                                    wait_tile(pe, r_used, s, g + back, before)
                                    nc.tensor.matmul(ps_r[:, r_bank[j], 0:384], hid[:, k, j * P:(j + 1) * P], r_w2[:, :],
                                                     start=True, stop=True).then_inc(r_made, 1)
                                behind = 1 if j < TILE_LAG else 0
                                if live(b, k, behind):
                                    sum_products(s, b, k, behind, (j - TILE_LAG) % GT)
                                if j == 3 and live(b, k, 3):
                                    z = slot(k, 3)
                                    wait_groups(pe, np_copied, s, g - 3 + 1)
                                    wait_groups(pe, side_made, s, g - 3 + 1)
                                    wait_groups(pe, out0_copied, s, g - 3 + 1)
                                    wait_groups(pe, sum_added, s, g - 3)
                                    for c in range(CH):
                                        nc.tensor.matmul(ps_sum[0:D, 0:W], sum16[:, c, :], node_prods[:, z, c, :],
                                                         start=(c == 0), stop=False)
                                    for i in range(GT):
                                        last = nc.tensor.matmul(ps_sum[0:D, 0:W], side[:, z, i, :], pick[:, z, i, :],
                                                                start=False, stop=(i == GT - 1))
                                    last.then_inc(sum_made, 1)

                @block.vector
                def _(dve):
                    nc.vector.memset(hid[RH:P, :, :], 0.0).then_inc(swept, 1)
                    sweeps = dve.value_load(sweeps_i[0:1, 0:1], min_val=1, max_val=256)
                    with dve.Fori(0, sweeps) as s:
                        dve.wait_ge(swept, s + 1)
                        for b, k in turns(dve, 4):
                            g = b * U + k

                            def products(lo, hi):
                                if not live(b, k, 1):
                                    return
                                z = slot(k, 1)
                                if lo == 0:
                                    wait_groups(dve, mix_made, s, g - 1 + 1)
                                    wait_groups(dve, vec_made, s, g - 1 + 1)
                                    wait_groups(dve, sum_made, s, g - 1 - U + 1)
                                wait_sums(dve, s, g - 2, 0 if hi <= SPLIT_SUMS else 1)
                                wait_tile(dve, r_made, s, g - 1, hi - 1)
                                wait_tile(dve, np_made, s, g - 2, hi - 1)
                                r = ps_r[:, r_bank[lo]:r_bank[lo] + hi - lo, :]
                                nc.vector.tensor_tensor(
                                    prods[:, lo:hi, 0:256].rearrange("p j (r s) -> p j r s", s=16),
                                    r[:, :, 0:256].rearrange("p j (r s) -> p j r s", s=16),
                                    spread(mix_in[:, z, lo:hi].rearrange("p j s v -> p j (s v)"), 2, 16), ALU.mult)
                                for j in range(lo, hi):
                                    nc.vector.tensor_tensor(
                                        prods[:, j, 256:640].rearrange("p (u o s) -> p u o s", u=MUL, o=3),
                                        spread(r[:, j - lo, 256:384].rearrange("p (u s) -> p u s", u=MUL), 2, 3),
                                        spread(vec_in[:, z, j].rearrange("p o t v -> p o (t v)"), 1, MUL), ALU.mult)\
                                        .then_inc(r_used, 1)

                            def sum_rows(lag, half):
                                if not live(b, k, lag):
                                    return
                                z = slot(k, lag)
                                lo, hi = ((0, SPLIT_SUMS), (SPLIT_SUMS, GT))[half]
                                wait_tile(dve, r_used, s, g - lag, hi - 1)
                                nc.vector.tensor_reduce(sums[:, z, lo:hi, :],
                                                        prods[:, lo:hi, 0:16 * ROWS].rearrange("p j (r s) -> p j r s", s=16),
                                                        AX.X, ALU.add).then_inc(summed, 1)

                            if live(b, k, 0):
                                wait_groups(dve, n5_made, s, g + 1)
                                wait_groups(dve, f_copied, s, g + 1)
                                wait_groups(dve, mix_made, s, g)
                                nc.vector.tensor_tensor(dots[:, :, :, :], f5[:, k, :, 0:3, :].rearrange("p j o v -> p j v o"),
                                                        spread(n5[:, k, :, 0:3], 2, MUL), ALU.mult).then_inc(dots_made, 1)
                            sum_rows(2, 1)
                            products(0, 2)
                            if live(b, k, 3):
                                z = slot(k, 3)
                                wait_groups(dve, along_made, s, g - 3 + 1)
                                more = side[:, z, :, MUL:ROWS - MUL]
                                nc.vector.tensor_tensor(more, more, sums[:, z, :, 2 * MUL:ROWS], ALU.add).then_inc(side_made, 1)
                            products(2, 4)
                            if live(b, k, 0):
                                wait_groups(dve, dots_made, s, g + 1)
                                nc.vector.tensor_reduce(mix_in[:, k, :, 1, :], dots[:, :, :, :], AX.X, ALU.add).then_inc(mix_made, 1)
                            sum_rows(1, 0)
                            if live(b, k, 4):
                                base = dve.value_load(base_i[0:1, bass.ds(g - 4, 1)], min_val=0, max_val=NODES)
                                wait_groups(dve, sum_made, s, g - 4 + 1)
                                wait_groups(dve, sum_added, s, g - 4)
                                nc.vector.tensor_tensor(acc[0:D, bass.ds(base, W)], acc[0:D, bass.ds(base, W)],
                                                        ps_sum[0:D, 0:W], ALU.add).then_inc(sum_added, 1)
                            products(4, 5)
                        wait_groups(dve, sum_added, s, GROUPS)
                        move_windows(dve, swept)

        node_step(True)


_INS = ["x", "src", "dst", "edge_attr_3", "edge_weight", "L0_gnn_W1", "L0_gnn_b1", "L0_gnn_W2", "L0_gnn_b2",
        "L0_gnn_W3", "L0_gnn_b3", "L0_gnn_W4", "L0_gnn_b4", "L1_gnn_w1", "L1_gnn_b1", "L1_gnn_w2", "L1_gnn_b2"]


def kernel(**inputs):
    import numpy as _np
    import concourse.bacc as _bacc
    from concourse import mybir as _mybir
    from concourse.bass_utils import run_bass_kernel_spmd as _run

    nc = _bacc.Bacc("TRN2", target_bir_lowering=False, num_devices=1)
    arrays, tensors = {}, {}
    for name in _INS:
        a = _np.ascontiguousarray(inputs[name])
        arrays[f"in_{name}_dram"] = a
        tensors[name] = nc.dram_tensor(f"in_{name}_dram", a.shape, _mybir.dt.from_np(a.dtype), kind="ExternalInput").ap()
    out = nc.dram_tensor("out_dram", (NODES, D), FP32, kind="ExternalOutput").ap()
    build(nc, tensors, out)
    r = _run(nc, [arrays], core_ids=[0])
    return r.results[0]["out_dram"]
```
